# Optimizing a Trainium2 kernel written in Bass

```python
import numpy as np
import jax
import jax.numpy as jnp

def _softmax(x, axis=-1):
    return jax.nn.softmax(x, axis=axis)

def _gelu(x):
    return jax.nn.gelu(x, approximate=True)

def _silu(x):
    return jax.nn.silu(x)

def _sigmoid(x):
    return jax.nn.sigmoid(x)

def _layernorm(x, axis=-1, eps=1e-05):
    m = jnp.mean(x, axis=axis, keepdims=True)
    v = jnp.var(x, axis=axis, keepdims=True)
    return (x - m) / jnp.sqrt(v + eps)

def _scatter_add(tgt, idx, src, axis=0):
    return tgt.at[idx].add(src)

def _segment_sum(src, seg, n):
    return jax.ops.segment_sum(src, seg, n)
kernel_name = 'mk_xattn_seq_d2_seqx_r4_44d6f7'

def setup_inputs(seed: int=0):
    np.random.seed(seed)
    _w = jnp.asarray

    def _rec_inputs():
        import jax
        import jax.numpy as jnp
        _rk = jax.random.key(seed)
        x = -0.0001548 + 1 * jax.random.normal(jax.random.fold_in(_rk, 1), (2, 512, 320), jnp.float32)
        _lenS = 512 - jax.random.randint(jax.random.fold_in(_rk, 7), (2,), 0, max(1, 512 // 4) + 1, jnp.int32)
        _lenS2 = 1024 - jax.random.randint(jax.random.fold_in(_rk, 8), (2,), 0, max(1, 1024 // 4) + 1, jnp.int32)
        _ctx_768P = jax.random.normal(jax.random.fold_in(_rk, 11), (2, 16, 192), jnp.float32)
        _ctx_768c = jax.random.dirichlet(jax.random.fold_in(_rk, 511), 0.3 * jnp.ones((16,), jnp.float32), (2, 1024))
        _ctx_768t = jnp.einsum('bsk,bkd->bsd', _ctx_768c, _ctx_768P)
        _ctx_768t = _ctx_768t * jax.lax.rsqrt(jnp.mean(jnp.square(_ctx_768t)) + 1e-12) * 0.953939
        ctx_768 = 0.00141353 + 0.998943 * (_ctx_768t + 0.3 * jax.random.normal(jax.random.fold_in(_rk, 611), (2, 1024, 192), jnp.float32))
        return (x, ctx_768)
    x, ctx_768 = _rec_inputs()

    def _L0_xattn_setup():
        import jax, jax.numpy as jnp
        import numpy as np
        HEADS = 8
        NUM_TOKENS = 4
        CROSS_ATTENTION_DIM = 192

        def _mha(q, k, v, heads=HEADS):
            B, Sq, H = q.shape
            Sk = k.shape[1]
            d = H // heads
            qh = q.reshape(B, Sq, heads, d).transpose(0, 2, 1, 3)
            kh = k.reshape(B, Sk, heads, d).transpose(0, 2, 1, 3)
            vh = v.reshape(B, Sk, heads, d).transpose(0, 2, 1, 3)
            scores = jnp.einsum('bhqd,bhkd->bhqk', qh, kh) * jnp.asarray(d, q.dtype) ** (-0.5)
            probs = jax.nn.softmax(scores, axis=-1)
            out = jnp.einsum('bhqk,bhkd->bhqd', probs, vh)
            return out.transpose(0, 2, 1, 3).reshape(B, Sq, H)
        key = jax.random.key(seed)
        ks = jax.random.split(key, 10)
        B, S, H, CAD, T = (4, 256, 320, CROSS_ATTENTION_DIM, NUM_TOKENS)
        sc = 0.02
        return {'hidden_states': jax.random.normal(ks[0], (B, S, H), jnp.float32), 'encoder_hidden_states': jax.random.normal(ks[1], (B, 77 + T, CAD), jnp.float32), 'Wq': jax.random.normal(ks[2], (H, H), jnp.float32) * sc, 'Wk': jax.random.normal(ks[3], (CAD, H), jnp.float32) * sc, 'Wv': jax.random.normal(ks[4], (CAD, H), jnp.float32) * sc, 'Wq_ca': jax.random.normal(ks[5], (T, H), jnp.float32) * sc, 'Wk_ca': jax.random.normal(ks[6], (CAD, H), jnp.float32) * sc, 'Wv_ca': jax.random.normal(ks[7], (CAD, H), jnp.float32) * sc, 'Wout': jax.random.normal(ks[8], (H, H), jnp.float32) * sc, 'b_out': jnp.zeros((H,), jnp.float32)}
    _L0_xattn_all = _L0_xattn_setup()
    _L0_xattn_in = {k: v for k, v in _L0_xattn_all.items() if k in ('Wq', 'Wk', 'Wv', 'Wq_ca', 'Wk_ca', 'Wv_ca', 'Wout', 'b_out')}
    del _L0_xattn_all

    def _L1_xattn_setup():
        import jax, jax.numpy as jnp
        import numpy as np
        D = 320
        H = 20
        DH = D // H
        CTX = 192
        FF_IN = 4 * D
        EPS = 1e-05

        def _ln(x, g, b):
            m = jnp.mean(x, axis=-1, keepdims=True)
            v = jnp.mean(jnp.square(x - m), axis=-1, keepdims=True)
            return (x - m) * jax.lax.rsqrt(v + EPS) * g + b

        def _attn(x, ctx, wq, wk, wv, wo, bo, heads):
            b, n, _ = x.shape
            j = ctx.shape[1]
            dh = wq.shape[1] // heads
            scale = dh ** (-0.5)
            q = (x @ wq).reshape(b, n, heads, dh).transpose(0, 2, 1, 3)
            k = (ctx @ wk).reshape(b, j, heads, dh).transpose(0, 2, 1, 3)
            v = (ctx @ wv).reshape(b, j, heads, dh).transpose(0, 2, 1, 3)
            sim = jnp.einsum('bhid,bhjd->bhij', q, k) * scale
            a = jax.nn.softmax(sim, axis=-1)
            out = jnp.einsum('bhij,bhjd->bhid', a, v)
            out = out.transpose(0, 2, 1, 3).reshape(b, n, heads * dh)
            return out @ wo + bo
        key = jax.random.key(seed)
        ks = jax.random.split(key, 24)
        r = lambda k, shp, s: jax.random.normal(k, shp, dtype=jnp.float32) * s
        d = {'x': r(ks[0], (8, 256, D), 1.0), 'context': r(ks[1], (8, 77, CTX), 1.0), 'heads': H, 'n1_g': jnp.ones((D,), jnp.float32), 'n1_b': jnp.zeros((D,), jnp.float32), 'q1': r(ks[2], (D, D), D ** (-0.5)), 'k1': r(ks[3], (D, D), D ** (-0.5)), 'v1': r(ks[4], (D, D), D ** (-0.5)), 'o1_w': r(ks[5], (D, D), D ** (-0.5)), 'o1_b': jnp.zeros((D,), jnp.float32), 'n2_g': jnp.ones((D,), jnp.float32), 'n2_b': jnp.zeros((D,), jnp.float32), 'q2': r(ks[6], (D, D), D ** (-0.5)), 'k2': r(ks[7], (CTX, D), CTX ** (-0.5)), 'v2': r(ks[8], (CTX, D), CTX ** (-0.5)), 'o2_w': r(ks[9], (D, D), D ** (-0.5)), 'o2_b': jnp.zeros((D,), jnp.float32), 'n3_g': jnp.ones((D,), jnp.float32), 'n3_b': jnp.zeros((D,), jnp.float32), 'ff_w1': r(ks[10], (D, 2 * FF_IN), D ** (-0.5)), 'ff_b1': jnp.zeros((2 * FF_IN,), jnp.float32), 'ff_w2': r(ks[11], (FF_IN, D), FF_IN ** (-0.5)), 'ff_b2': jnp.zeros((D,), jnp.float32)}
        return d
    _L1_xattn_all = _L1_xattn_setup()
    _L1_xattn_in = {k: v for k, v in _L1_xattn_all.items() if k in ('n1_g', 'n1_b', 'q1', 'k1', 'v1', 'o1_w', 'o1_b', 'n2_g', 'n2_b', 'q2', 'k2', 'v2', 'o2_w', 'o2_b', 'n3_g', 'n3_b', 'ff_w1', 'ff_b1', 'ff_w2', 'ff_b2')}
    del _L1_xattn_all
    return {'x': x, 'ctx_768': ctx_768, 'L0_xattn_Wq': _L0_xattn_in['Wq'], 'L0_xattn_Wk': _L0_xattn_in['Wk'], 'L0_xattn_Wv': _L0_xattn_in['Wv'], 'L0_xattn_Wq_ca': _L0_xattn_in['Wq_ca'], 'L0_xattn_Wk_ca': _L0_xattn_in['Wk_ca'], 'L0_xattn_Wv_ca': _L0_xattn_in['Wv_ca'], 'L0_xattn_Wout': _L0_xattn_in['Wout'], 'L0_xattn_b_out': _L0_xattn_in['b_out'], 'L1_xattn_n1_g': _L1_xattn_in['n1_g'], 'L1_xattn_n1_b': _L1_xattn_in['n1_b'], 'L1_xattn_q1': _L1_xattn_in['q1'], 'L1_xattn_k1': _L1_xattn_in['k1'], 'L1_xattn_v1': _L1_xattn_in['v1'], 'L1_xattn_o1_w': _L1_xattn_in['o1_w'], 'L1_xattn_o1_b': _L1_xattn_in['o1_b'], 'L1_xattn_n2_g': _L1_xattn_in['n2_g'], 'L1_xattn_n2_b': _L1_xattn_in['n2_b'], 'L1_xattn_q2': _L1_xattn_in['q2'], 'L1_xattn_k2': _L1_xattn_in['k2'], 'L1_xattn_v2': _L1_xattn_in['v2'], 'L1_xattn_o2_w': _L1_xattn_in['o2_w'], 'L1_xattn_o2_b': _L1_xattn_in['o2_b'], 'L1_xattn_n3_g': _L1_xattn_in['n3_g'], 'L1_xattn_n3_b': _L1_xattn_in['n3_b'], 'L1_xattn_ff_w1': _L1_xattn_in['ff_w1'], 'L1_xattn_ff_b1': _L1_xattn_in['ff_b1'], 'L1_xattn_ff_w2': _L1_xattn_in['ff_w2'], 'L1_xattn_ff_b2': _L1_xattn_in['ff_b2']}

def reference(x, ctx_768, L0_xattn_Wq, L0_xattn_Wk, L0_xattn_Wv, L0_xattn_Wq_ca, L0_xattn_Wk_ca, L0_xattn_Wv_ca, L0_xattn_Wout, L0_xattn_b_out, L1_xattn_n1_g, L1_xattn_n1_b, L1_xattn_q1, L1_xattn_k1, L1_xattn_v1, L1_xattn_o1_w, L1_xattn_o1_b, L1_xattn_n2_g, L1_xattn_n2_b, L1_xattn_q2, L1_xattn_k2, L1_xattn_v2, L1_xattn_o2_w, L1_xattn_o2_b, L1_xattn_n3_g, L1_xattn_n3_b, L1_xattn_ff_w1, L1_xattn_ff_b1, L1_xattn_ff_w2, L1_xattn_ff_b2):
    import jax
    import jax.numpy as jnp

    def _L0_xattn_ref(hidden_states, encoder_hidden_states, Wq, Wk, Wv, Wq_ca, Wk_ca, Wv_ca, Wout, b_out):
        import jax, jax.numpy as jnp
        import numpy as np
        HEADS = 8
        NUM_TOKENS = 4
        CROSS_ATTENTION_DIM = 192

        def _mha(q, k, v, heads=HEADS):
            B, Sq, H = q.shape
            Sk = k.shape[1]
            d = H // heads
            qh = q.reshape(B, Sq, heads, d).transpose(0, 2, 1, 3)
            kh = k.reshape(B, Sk, heads, d).transpose(0, 2, 1, 3)
            vh = v.reshape(B, Sk, heads, d).transpose(0, 2, 1, 3)
            scores = jnp.einsum('bhqd,bhkd->bhqk', qh, kh) * jnp.asarray(d, q.dtype) ** (-0.5)
            probs = jax.nn.softmax(scores, axis=-1)
            out = jnp.einsum('bhqk,bhkd->bhqd', probs, vh)
            return out.transpose(0, 2, 1, 3).reshape(B, Sq, H)
        residual = hidden_states
        unet_size = residual.shape[1]
        end_pos = encoder_hidden_states.shape[1] - NUM_TOKENS
        enc = encoder_hidden_states[:, :end_pos, :]
        ca = encoder_hidden_states[:, end_pos:, :]
        query = hidden_states @ Wq
        keyt = enc @ Wk
        valt = enc @ Wv
        hs = _mha(query, keyt, valt)
        ca_q1 = jnp.einsum('btc,th->bch', ca, Wq_ca)
        indices = np.linspace(0, CROSS_ATTENTION_DIM - 1, unet_size).astype(np.int64)
        ca_q1 = ca_q1[:, indices, :]
        ca_hs1 = _mha(ca_q1, residual, residual)
        ca_q2 = ca_hs1 @ Wq
        ca_k2 = ca @ Wk_ca
        ca_v2 = ca @ Wv_ca
        ca_hs2 = _mha(ca_q2, ca_k2, ca_v2)
        out = hs + ca_hs2
        out = out @ Wout + b_out
        out = out + residual
        return out

    def _L1_xattn_ref(x, context, heads, n1_g, n1_b, q1, k1, v1, o1_w, o1_b, n2_g, n2_b, q2, k2, v2, o2_w, o2_b, n3_g, n3_b, ff_w1, ff_b1, ff_w2, ff_b2):
        import jax, jax.numpy as jnp
        import numpy as np
        D = 320
        H = 20
        DH = D // H
        CTX = 192
        FF_IN = 4 * D
        EPS = 1e-05

        def _ln(x, g, b):
            m = jnp.mean(x, axis=-1, keepdims=True)
            v = jnp.mean(jnp.square(x - m), axis=-1, keepdims=True)
            return (x - m) * jax.lax.rsqrt(v + EPS) * g + b

        def _attn(x, ctx, wq, wk, wv, wo, bo, heads):
            b, n, _ = x.shape
            j = ctx.shape[1]
            dh = wq.shape[1] // heads
            scale = dh ** (-0.5)
            q = (x @ wq).reshape(b, n, heads, dh).transpose(0, 2, 1, 3)
            k = (ctx @ wk).reshape(b, j, heads, dh).transpose(0, 2, 1, 3)
            v = (ctx @ wv).reshape(b, j, heads, dh).transpose(0, 2, 1, 3)
            sim = jnp.einsum('bhid,bhjd->bhij', q, k) * scale
            a = jax.nn.softmax(sim, axis=-1)
            out = jnp.einsum('bhij,bhjd->bhid', a, v)
            out = out.transpose(0, 2, 1, 3).reshape(b, n, heads * dh)
            return out @ wo + bo
        h1 = _ln(x, n1_g, n1_b)
        x = _attn(h1, h1, q1, k1, v1, o1_w, o1_b, heads) + x
        h2 = _ln(x, n2_g, n2_b)
        x = _attn(h2, context, q2, k2, v2, o2_w, o2_b, heads) + x
        h3 = _ln(x, n3_g, n3_b)
        proj = h3 @ ff_w1 + ff_b1
        a, g = jnp.split(proj, 2, axis=-1)
        ff = a * jax.nn.gelu(g, approximate=False) @ ff_w2 + ff_b2
        return ff + x
    x = _L0_xattn_ref(x, ctx_768, L0_xattn_Wq, L0_xattn_Wk, L0_xattn_Wv, L0_xattn_Wq_ca, L0_xattn_Wk_ca, L0_xattn_Wv_ca, L0_xattn_Wout, L0_xattn_b_out)
    x = _L1_xattn_ref(x, ctx_768, 20, L1_xattn_n1_g, L1_xattn_n1_b, L1_xattn_q1, L1_xattn_k1, L1_xattn_v1, L1_xattn_o1_w, L1_xattn_o1_b, L1_xattn_n2_g, L1_xattn_n2_b, L1_xattn_q2, L1_xattn_k2, L1_xattn_v2, L1_xattn_o2_w, L1_xattn_o2_b, L1_xattn_n3_g, L1_xattn_n3_b, L1_xattn_ff_w1, L1_xattn_ff_b1, L1_xattn_ff_w2, L1_xattn_ff_b2)
    return x

_drawn_inputs = setup_inputs


def setup_inputs(seed=0):
    import zlib

    import numpy as np

    out = dict(_drawn_inputs(seed))
    spreads = {'L0_xattn_b_out': (0.0, 0.1),
     'L1_xattn_n1_g': (1.0, 0.2),
     'L1_xattn_n1_b': (0.0, 0.1),
     'L1_xattn_o1_b': (0.0, 0.1),
     'L1_xattn_n2_g': (1.0, 0.2),
     'L1_xattn_n2_b': (0.0, 0.387),
     'L1_xattn_o2_b': (0.0, 0.1),
     'L1_xattn_n3_g': (1.0, 0.2),
     'L1_xattn_n3_b': (0.0, 0.1),
     'L1_xattn_ff_b1': (0.0, 0.1),
     'L1_xattn_ff_b2': (0.0, 0.1)}
    factors = {'L0_xattn_Wq': 8.0, 'L0_xattn_Wk': 8.0, 'L0_xattn_Wq_ca': 43.706, 'L0_xattn_Wk_ca': 26.742}
    for name, (base, spread) in spreads.items():
        noise = np.random.default_rng([zlib.crc32(name.encode()), seed]).standard_normal(out[name].shape)
        drawn = base * np.exp(spread * noise) if base else spread * noise
        out[name] = jnp.asarray(drawn.astype(out[name].dtype))
    for name, factor in factors.items():
        out[name] = (out[name] * factor).astype(out[name].dtype)
    return out
```

```python
import numpy as np
import concourse.bass as bass
from concourse import mybir

F32 = mybir.dt.float32
F32R = mybir.dt.float32r
ALU = mybir.AluOpType
ACT = mybir.ActivationFunctionType
AX = mybir.AxisListType

B, SQ, D = 2, 512, 320
SK, DC = 1024, 192
TOK = B * SQ
TT = TOK // 128
FTILES = [(0, 128), (128, 128), (256, 64)]
KF = len(FTILES)
CT, CP = 2, 96
NCA = 4
UQ = DC
H0, D0 = 8, 40
H1, D1 = 20, 16
FF = 4 * D
FT = FF // 128
EPS = 1e-5
RING = 4
PRING = 4
SBANKS = (4, 5, 6)
SPREAD = {1: ((0, 3), (3, 4)), 2: ((0, 1), (1, 3), (3, 4))}
OBANK = 7


class Attention:

    def __init__(self, name, heads, d, width, terms_q, terms_k, nq, qt, keys, lead):
        self.name, self.heads, self.d = name, heads, d
        self.width = width
        self.g = 128 // width
        self.pairs = self.g // 2
        self.groups = B * heads // self.g
        self.terms_q, self.terms_k = terms_q, terms_k
        self.rows = max(96, d * len(terms_q))
        self.nq, self.qt, self.nqt = nq, qt, nq // qt
        self.keys = keys
        self.kt = -(-keys // 128)
        self.size = [min(128, keys - 128 * t) for t in range(self.kt)]
        self.chunks = [(c, min(512, keys - c)) for c in range(0, keys, 512)]
        self.items = [(j, q, c) for j in range(self.g) for q in range(self.nqt) for c in range(len(self.chunks))]
        self.per_step = len(self.items) // self.kt
        self.lead = lead
        self.cols = self.g * self.nqt
        self.scale = float(d) ** -0.5
        self.shift = 1
        span = (lead + self.shift + self.kt - 1) // self.kt
        self.loops = (self.groups - span) // 3
        assert self.kt < lead < 2 * self.kt + 1 and len(self.items) % self.kt == 0


HH_L = (0, 0, 1)
H_LH = (0, 1, 0)
HHLL = (0, 0, 1, 1)
HLHL = (0, 1, 0, 1)
A_MAIN = Attention("main", H0, D0, 64, HH_L, H_LH, SQ, 128, SK - NCA, 13)
A_CA = Attention("ca", H0, D0, 64, HH_L, H_LH, UQ, 96, SQ, 8)
A_SELF = Attention("self", H1, D1, 32, HHLL, HLHL, SQ, 128, SQ, 7)
A_CROSS = Attention("cross", H1, D1, 32, HHLL, HLHL, SQ, 128, SK, 12)


class At:

    def __init__(self, loop, off):
        self.loop, self.off = loop, off
        self.slot = off % 3

    def plus(self, k):
        return At(self.loop, self.off + k)

    def times(self, per, k=0):
        return self.loop * (3 * per) + (self.off * per + k)

    def turn(self, per, k=0):
        return self.loop * per + ((self.off // 3 + 1) * per + k)


def build(nc, ins, out_dram):
    at = [16512]

    def place(name, shape, dt=F32, offset=None):
        size = int(np.prod(shape[1:])) * 4
        if offset is None:
            offset = at[0]
            at[0] += -(-size // 32) * 32
        return nc.alloc_sbuf_tensor_at(name, shape, dt, offset=offset)

    def region(size):
        start = at[0]
        at[0] += size
        return start

    ident = place("ident", [128, 128])
    params = place("params", [128, 38])
    brows = place("brows", [128, 4, D])
    onehot = place("onehot", [CP, 2, SQ])
    hmask = place("hmask", [128, KF, H0 * NCA])
    w_s0 = place("w_s0", [128, KF, D])
    w_s1 = place("w_s1", [128, KF, D])
    w_s2 = place("w_s2", [128, KF, D])
    w_pad_a = place("w_pad_a", [128, 5, D])
    w_pad_b = place("w_pad_b", [128, 5, D])
    act_t = place("act_t", [128, KF, TOK])
    resid = place("resid", [128, TT, D])
    r1 = region(max(16384 + 4 * 2560 + 2 * 2560, 20480 + 6144))
    ctx_t = place("ctx_t", [CP, CT, B * SK], offset=r1)
    w_k0 = place("w_k0", [CP, CT, D], offset=r1 + 16384)
    w_v0 = place("w_v0", [CP, CT, D], offset=r1 + 18944)
    w_k2 = place("w_k2", [CP, CT, D], offset=r1 + 21504)
    w_v2 = place("w_v2", [CP, CT, D], offset=r1 + 24064)
    w_kca = place("w_kca", [CP, CT, D], offset=r1 + 26624)
    w_vca = place("w_vca", [CP, CT, D], offset=r1 + 29184)
    out_t = place("out_t", [128, 10, SQ], offset=r1)
    ca_t = place("ca_t", [128, 8, UQ], offset=r1 + 20480)
    r2 = region(3 * 8192 + 3 * 16384 + 3 * 4096 + PRING * 4096)
    q_st = [place(f"q_st{s}", [128, 2048], F32R, offset=r2 + 8192 * s) for s in range(3)]
    k_st = [place(f"k_st{s}", [128, 4096], F32R, offset=r2 + 24576 + 16384 * s) for s in range(3)]
    v_st = [place(f"v_st{s}", [128, 8, 128], F32, offset=r2 + 73728 + 4096 * s) for s in range(3)]
    probs = place("probs", [128, PRING, 2, SQ], F32, offset=r2 + 86016)
    w_ff1 = place("w_ff1", [128, KF, 2 * FF], F32, offset=r2)
    w_ff2 = place("w_ff2", [128, FT, D], F32, offset=r2 + 30720)
    ff_t = place("ff_t", [128, FT, TOK], F32, offset=r2 + 43520)
    gelu = place("gelu", [128, 2, SQ], F32, offset=r2 + 84480)
    split = place("split", [128, RING, 2, SQ], F32R, offset=r2 + 86016)
    r4 = region(4096)
    vpad0 = place("vpad0", [128, 2, H0, 64], offset=r4)
    ep3 = place("ep3", [32, B, SQ], offset=r4)
    vpad1 = place("vpad1", [128, 2, H1, 32])
    maxp = place("maxp", [128, 3, 32])
    negm = place("negm", [128, 3, 16])
    msplit = place("msplit", [16, 3, 2, 128], F32R)
    r5 = region(2048)
    turned = place("turned", [128, SQ], offset=r5)
    back = place("back", [128, SQ])
    recip = place("recip", [128, 32])
    ca_nat = place("ca_nat", [NCA, B, DC], offset=r5)
    r6 = region(2560)
    xhat = place("xhat", [128, 2, D], offset=r6)
    wqca = place("wqca", [NCA, D], offset=r6)
    q2t = place("q2t", [128, KF, UQ], offset=r6)
    stats = place("stats", [128, 6])
    mv = place("mv", [128, TT, 2])
    rstd = place("rstd", [128, TT])
    std = place("std", [128, TT])
    eps = place("eps", [128, 1])
    kbd = place("kbd", [128, B, KF, H0, NCA])
    vbd = place("vbd", [128, B, KF, H0, NCA])
    vw = place("vw", [32, B, D], offset=r1 + 26624)
    p3 = place("p3", [CP, B, 2, 32], offset=r1 + 29184)
    s3 = place("s3", [CP, 2, 32], offset=r1 + 29696)
    assert at[0] <= 229344, at[0]
    PS = nc.alloc_psum_tensor("PS", [128, 8, 512], F32)

    def dram(name, shape):
        return nc.dram_tensor(name, shape, F32, kind="Internal").ap()

    q0_d, x0_d = dram("q0_d", [2, B * D, SQ]), dram("x0_d", [2, B * D, SQ])
    k0_d, cq_d = dram("k0_d", [2, B * D, SK]), dram("cq_d", [2, B * D, UQ])
    q1_d, k1_d = dram("q1_d", [2, B * D, SQ]), dram("k1_d", [2, B * D, SQ])
    q2_d, k2_d = dram("q2_d", [2, B * D, SQ]), dram("k2_d", [2, B * D, SK])
    v0_d, vx_d = dram("v0_d", [8, 128, 8, 128]), dram("vx_d", [8, 128, 4, 128])
    v1_d, v2_d = dram("v1_d", [10, 128, 4, 128]), dram("v2_d", [10, 128, 8, 128])

    count = [0]

    def sem(name):
        count[0] += 1
        return nc.alloc_semaphore(name)

    loads = {
        "a": [(act_t, "x_t"), (w_s0, "Wq")],
        "c": [(ctx_t, "ctx_t"), (w_k0, "Wk"), (wqca, "Wq_ca"), (ca_nat, "ca"), (w_v0, "Wv"), (resid, "x")],
        "b": [(w_k2, "k2"), (w_v2, "v2"), (w_kca, "Wk_ca"), (w_vca, "Wv_ca"), (w_s1, "Wout"),
              (hmask, "hmask"), (ident, "ident"), (onehot, "onehot"),
              (params, "params"), (w_pad_a, "Wout_g"), (w_pad_b, "Wq_g"), (w_s2, "v1")],
    }
    loaded_a, loaded_c, loaded_b = sem("loaded_a"), sem("loaded_c"), sem("loaded_b")
    ALL_A, ALL_C, ALL_B = 16 * len(loads["a"]), 16 * len(loads["c"]), 16 * (len(loads["b"]) + 1)

    def rows_of(dst, b, m, c, n):
        f0, fn = FTILES[m]
        return dst[:, b * D + f0:b * D + f0 + fn, c:c + n].rearrange("t f n -> f t n")

    def feat_job(w, parts, ktiles, src, m, b, c, n, dst):
        f0, fn = FTILES[m]
        return dict(kind="s", mm=[(w[0:p, k, f0:f0 + fn], src(k, p)) for k, p in zip(range(ktiles), parts)],
                    m=fn, n=n, src=None, dst=rows_of(dst, b, m, c, n))

    XP = [128, 128, 64]
    CPS = [CP, CP]

    def x_cols(b):
        return lambda k, p: act_t[0:p, k, b * SQ:(b + 1) * SQ]

    def c_cols(b, c):
        return lambda k, p: ctx_t[0:p, k, b * SK + c:b * SK + c + 512]

    def v_job(mm, layer, dst, b, t):
        return dict(kind="v", mm=mm, layer=layer, src=None,
                    dst=dst[b * (4 if layer == 0 else 5):(b + 1) * (4 if layer == 0 else 5), :, t, :]
                    .rearrange("g p c -> p g c"))

    C_FROM = 2 * B * KF
    B_FROM = C_FROM + B * (2 * KF + KF + 8 + 4)

    def first_jobs():
        jobs = []
        for b in range(B):
            jobs += [feat_job(w_s0, XP, KF, x_cols(b), m, b, 0, SQ, q0_d) for m in range(KF)]
            jobs += [dict(kind="s", mm=None, m=FTILES[m][1], n=SQ, src=x_cols(b)(m, FTILES[m][1]),
                          dst=rows_of(x0_d, b, m, 0, SQ)) for m in range(KF)]
        for b in range(B):
            for c in (0, 512):
                jobs += [feat_job(w_k0, CPS, CT, c_cols(b, c), m, b, c, 512, k0_d) for m in range(KF)]
            jobs += [dict(kind="s", mm=[(wqca[:, FTILES[m][0]:FTILES[m][0] + FTILES[m][1]], ca_nat[:, b, :])],
                          m=FTILES[m][1], n=UQ, src=None, dst=rows_of(cq_d, b, m, 0, UQ)) for m in range(KF)]
            for t in range(8):
                jobs.append(v_job([(ctx_t[0:CP, k, b * SK + t * 128:b * SK + t * 128 + 128], w_v0[0:CP, k, :])
                                   for k in range(CT)], 0, v0_d, b, t))
            for t in range(4):
                j = v_job(None, 0, vx_d, b, t)
                j["src"] = resid[:, b * 4 + t, :]
                jobs.append(j)
        for b in range(B):
            for c in (0, 512):
                jobs += [feat_job(w_k2, CPS, CT, c_cols(b, c), m, b, c, 512, k2_d) for m in range(KF)]
            for t in range(8):
                jobs.append(v_job([(ctx_t[0:CP, k, b * SK + t * 128:b * SK + t * 128 + 128], w_v2[0:CP, k, :])
                                   for k in range(CT)], 1, v2_d, b, t))
        return jobs

    def self_jobs():
        jobs = []
        for b in range(B):
            for m in range(KF):
                jobs.append(feat_job(w_s0, XP, KF, x_cols(b), m, b, 0, SQ, q1_d))
                jobs.append(feat_job(w_s1, XP, KF, x_cols(b), m, b, 0, SQ, k1_d))
            for t in range(4):
                jobs.append(v_job([(act_t[0:p, k, (b * 4 + t) * 128:(b * 4 + t + 1) * 128], w_s2[0:p, k, :])
                                   for k, p in enumerate(XP)], 1, v1_d, b, t))
        return jobs

    def cross_jobs():
        return [feat_job(w_s0, XP, KF, x_cols(b), m, b, 0, SQ, q2_d) for b in range(B) for m in range(KF)]

    class Projection:
        def __init__(self, name, jobs):
            self.jobs, ns, nv, nm = [], 0, 0, 0
            for at_, j in enumerate(jobs):
                j["at"] = at_
                if j["kind"] == "s":
                    j["i"], ns = ns, ns + 1
                    if j["mm"]:
                        nm += 1
                        j["mm_count"] = nm
                else:
                    j["i"], nv = nv, nv + 1
                    if j["mm"]:
                        nm += 1
                        j["mm_count"] = nm
                self.jobs.append(j)
            self.ns, self.nv = ns, nv
            self.product = sem(name + "_product")
            self.high = sem(name + "_high")
            self.low = sem(name + "_low")
            self.padded = sem(name + "_padded")
            self.stored = [sem(f"{name}_stored{s}") for s in range(RING)]
            self.vstored = [sem(f"{name}_vstored{s}") for s in range(2)]

        def wait_stored(self, eng):
            for s in range(RING):
                n = len(range(s, self.ns, RING))
                if n:
                    eng.wait_ge(self.stored[s], 16 * n)
            for s in range(2):
                n = len(range(s, self.nv, 2))
                if n:
                    eng.wait_ge(self.vstored[s], 16 * n)

    first = Projection("first", first_jobs())
    selfp = Projection("selfp", self_jobs())
    crossp = Projection("crossp", cross_jobs())

    def split_bank(j):
        return PS[0:j["m"], j["i"] % RING, 0:j["n"]]

    def value_bank(j):
        return PS[:, 4 + j["i"] % 2, 0:D]

    def inputs_in(eng, ph, j):
        if ph is first:
            if j["at"] == C_FROM:
                eng.wait_ge(loaded_c, ALL_C)
            if j["at"] == B_FROM:
                eng.wait_ge(loaded_b, ALL_B)

    def pe_projection(pe, ph):
        for j in ph.jobs:
            inputs_in(pe, ph, j)
            if not j["mm"]:
                continue
            if j["kind"] == "s":
                if j["i"] >= RING:
                    pe.wait_ge(ph.low, j["i"] - RING + 1)
                o = split_bank(j)
            else:
                if j["i"] >= 2:
                    pe.wait_ge(ph.padded, j["i"] - 2 + 1)
                o = value_bank(j)
            for k, (w, a) in enumerate(j["mm"]):
                mm = nc.tensor.matmul(o, w, a, start=(k == 0), stop=(k == len(j["mm"]) - 1))
            mm.then_inc(ph.product, 1)

    def act_projection(act, ph):
        for j in ph.jobs:
            inputs_in(act, ph, j)
            if j["mm"]:
                act.wait_ge(ph.product, j["mm_count"])
            i = j["i"]
            if j["kind"] == "s":
                if i >= RING:
                    act.wait_ge(ph.stored[i % RING], 16 * (i // RING))
                nc.scalar.copy(split[0:j["m"], i % RING, 0, 0:j["n"]],
                               split_bank(j) if j["mm"] else j["src"]).then_inc(ph.high, 1)
            else:
                if i >= 2:
                    act.wait_ge(ph.vstored[i % 2], 16 * (i // 2))
                s = value_bank(j) if j["mm"] else j["src"]
                if j["layer"] == 0:
                    v = s.rearrange("p (h d) -> p h d", d=D0)
                    nc.scalar.copy(vpad0[:, i % 2, :, 0:31], v[:, :, 0:31])
                    nc.scalar.copy(vpad0[:, i % 2, :, 32:41], v[:, :, 31:40]).then_inc(ph.padded, 1)
                else:
                    nc.scalar.copy(vpad1[:, i % 2, :, 0:D1],
                                   s.rearrange("p (h d) -> p h d", d=D1)).then_inc(ph.padded, 1)

    def dve_projection(dve, ph):
        for j in ph.jobs:
            if j["kind"] == "s":
                i = j["i"]
                dve.wait_ge(ph.high, i + 1)
                nc.vector.tensor_tensor(split[0:j["m"], i % RING, 1, 0:j["n"]],
                                        split_bank(j) if j["mm"] else j["src"],
                                        split[0:j["m"], i % RING, 0, 0:j["n"]].bitcast(F32),
                                        ALU.subtract).then_inc(ph.low, 1)

    def sp_projection(sp, ph):
        for j in ph.jobs:
            i = j["i"]
            if j["kind"] == "s":
                sp.wait_ge(ph.low, i + 1)
                sp.dma_start(j["dst"], split[0:j["m"], i % RING, :, 0:j["n"]].bitcast(F32)).then_inc(
                    ph.stored[i % RING], 16)
            else:
                sp.wait_ge(ph.padded, i + 1)
                pad = vpad0 if j["layer"] == 0 else vpad1
                sp.dma_start(j["dst"], pad[:, i % 2, :, :].rearrange("p h w -> p (h w)").rearrange(
                    "p (g c) -> p g c", c=128)).then_inc(ph.vstored[i % 2], 16)

    for a, (qd, kd, vd, dest) in ((A_MAIN, (q0_d, k0_d, v0_d, out_t)), (A_CA, (cq_d, x0_d, vx_d, ca_t)),
                                  (A_SELF, (q1_d, k1_d, v1_d, out_t)), (A_CROSS, (q2_d, k2_d, v2_d, out_t))):
        a.qd, a.kd, a.vd, a.dest = qd, kd, vd, dest
        n = a.name
        a.qk_loaded = [sem(f"{n}_qk_loaded{s}") for s in range(3)]
        a.v_loaded = [sem(f"{n}_v_loaded{s}") for s in range(3)]
        a.m_loaded = [sem(f"{n}_m_loaded{s}") for s in range(3)]
        a.score = sem(f"{n}_score")
        a.score_free = sem(f"{n}_score_free")
        a.neg_ready = sem(f"{n}_neg_ready")
        a.m_high = sem(f"{n}_m_high")
        a.pair = sem(f"{n}_pair")
        a.exp = sem(f"{n}_exp")
        a.used = sem(f"{n}_used")
        a.out_read = sem(f"{n}_out_read")
        a.norm = sem(f"{n}_norm")
        a.out_back = sem(f"{n}_out_back")
        a.out_done = sem(f"{n}_out_done")

    A_MAIN.ones, A_SELF.ones = sem("main_ones"), sem("self_ones")

    def q_view(a, s):
        return q_st[s][:, 0:a.g * a.nq].rearrange("p (j n) -> p j n", j=a.g)

    def k_view(a, s):
        kw = SK if a.keys > SQ else SQ
        return k_st[s][:, 0:a.g * kw].rearrange("p (j n) -> p j n", j=a.g)

    def item_index(a, g, i):
        if isinstance(g.loop, int) and g.loop * 3 + g.off == 0:
            return i, i % 3
        k = i - 1 + (1 if i >= a.per_step else 0)
        per = len(a.items) + 1
        return g.times(per, k), (g.off * per + k) % 3

    def flip_index(a, g):
        per = len(a.items) + 1
        last = isinstance(g.loop, int) and g.loop * 3 + g.off == a.groups - 1
        k = per - 1 + (0 if last else a.per_step)
        return g.times(per, k), (g.off * per + k) % 3

    def max_step(a, g, t):
        n = g.loop * 3 + g.off if isinstance(g.loop, int) else None
        ended = g.plus(-1) if t == 0 and n != 0 and (n is None or n <= a.groups) else None
        if n is not None and n >= a.groups:
            return (ended if n == a.groups else None), []
        return ended, [(i, a.items[i]) for i in range(t * a.per_step, (t + 1) * a.per_step)]

    def ahead(a, g, t):
        return g.plus((t + a.lead) // a.kt), (t + a.lead) % a.kt

    def run_groups(eng, a, body):
        with eng.Fori(0, a.loops) as r:
            for u in range(3):
                body(At(r, u))
        for n in range(3 * a.loops, a.groups):
            body(At(n // 3, n % 3))

    def sp_attention(sp, a, before, previous):
        before.wait_stored(sp)
        if a is A_MAIN:
            sp.wait_ge(a.ones, 1)
        if a is A_SELF:
            sp.wait_ge(a.ones, 2)
        kw = SK if a.keys > SQ else SQ
        rows = a.g * a.d

        def load_qk(g):
            r0 = g.times(rows)
            s = g.slot
            for t, part in enumerate(a.terms_q):
                sp.dma_start(q_view(a, s)[t * a.d:(t + 1) * a.d, :, :].bitcast(F32),
                             a.qd[part, bass.ds(r0, rows), 0:a.nq].rearrange("(j d) n -> d j n", j=a.g)).then_inc(
                    a.qk_loaded[s], 16)
            for t, part in enumerate(a.terms_k):
                sp.dma_start(k_view(a, s)[t * a.d:(t + 1) * a.d, :, :].bitcast(F32),
                             a.kd[part, bass.ds(r0, rows), 0:kw].rearrange("(j d) n -> d j n", j=a.g)).then_inc(
                    a.qk_loaded[s], 16)

        def load_v(g):
            n = g.times(1)
            sp.dma_start(v_st[g.slot][:, 0:a.kt, :],
                         a.vd[bass.ds(n, 1), :, 0:a.kt, :].rearrange("o p t c -> (o p) t c")).then_inc(
                a.v_loaded[g.slot], 16)

        def load_m(g):
            sp.wait_ge(a.score_free, 3 + flip_index(a, g)[0] + 1)
            for part in range(2):
                sp.dma_start(q_st[g.slot][a.rows + part:a.rows + part + 1, 0:a.g * a.nq].bitcast(F32).rearrange(
                    "o (c n) -> o c n", n=a.qt), msplit[0:a.cols, g.slot, part, 0:a.qt].bitcast(F32)).then_inc(
                    a.m_loaded[g.slot], 16)

        for n in range(3):
            if previous is not None:
                last = max(x for x in range(previous.groups) if x % 3 == n) + 1
                steps = previous.kt * previous.pairs
                sp.wait_ge(previous.pair, last * steps)
            load_qk(At(n // 3, n % 3))
            if previous is not None:
                sp.wait_ge(previous.used, PRING + last * steps)
            load_v(At(n // 3, n % 3))
        load_m(At(0, 0))

        def body(g):
            load_m(g.plus(1))
            sp.wait_ge(a.pair, g.times(a.kt * a.pairs, a.kt * a.pairs))
            load_qk(g.plus(3))
            sp.wait_ge(a.used, g.times(a.kt * a.pairs, PRING + a.kt * a.pairs))
            load_v(g.plus(3))

        loops = (a.groups - 3) // 3
        with sp.Fori(0, loops) as r:
            for u in range(3):
                body(At(r, u))
        for n in range(3 * loops, a.groups - 1):
            if n + 3 < a.groups:
                body(At(n // 3, n % 3))
            else:
                load_m(At((n + 1) // 3, (n + 1) % 3))

    def pe_attention(pe, a):
        steps = a.kt * a.pairs
        pe.sem_inc(a.used, PRING)

        def item(g, i, j, q, c):
            k, bank = item_index(a, g, i)
            if i == 0:
                pe.wait_ge(a.qk_loaded[g.slot], g.turn(16 * 2 * len(a.terms_q)))
            pe.wait_ge(a.score_free, k + 1)
            c0, cn = a.chunks[c]
            nc.tensor.matmul(PS[0:a.qt, SBANKS[bank], 0:cn],
                             q_view(a, g.slot)[0:a.rows, j, q * a.qt:(q + 1) * a.qt],
                             k_view(a, g.slot)[0:a.rows, j, c0:c0 + cn],
                             start=True, stop=True).then_inc(a.score, 1)

        def flip(ended):
            k, bank = flip_index(a, ended)
            pe.wait_ge(a.neg_ready, ended.times(1, 1))
            pe.wait_ge(a.score_free, k + 1)
            nc.tensor.transpose(PS[0:a.cols, SBANKS[bank], 0:a.qt],
                                negm[0:a.qt, ended.slot, 0:a.cols],
                                ident[0:a.qt, 0:a.qt]).then_inc(a.score, 1)

        def maxima(g, t, lo=0, hi=4):
            ended, items = max_step(a, g, t)
            start, stop = -(-lo * len(items) // 4), -(-hi * len(items) // 4)
            for i, jqc in items[start:stop]:
                item(g, i, *jqc)
            if ended is not None and (hi == 4 if items else lo == 0):
                flip(ended)

        def scores(g, t, p):
            sz = a.size[t]
            if t == 0 and p == 0:
                pe.wait_ge(a.m_loaded[g.slot], g.turn(32))
            q = g.times(steps, t * a.pairs + p)
            bank = 2 * ((g.off * steps + t * a.pairs + p) % 2)
            pe.wait_ge(a.exp, q + 1)
            for half in range(2):
                j = 2 * p + half
                mm = nc.tensor.matmul(PS[0:sz, bank + half, 0:a.nq],
                                      k_view(a, g.slot)[0:a.rows + 2, j, t * 128:t * 128 + sz],
                                      q_view(a, g.slot)[0:a.rows + 2, j, :], start=True, stop=True)
            mm.then_inc(a.pair, 1)

        def values(g, t, p):
            sz, w = a.size[t], a.width
            if t == 0 and p == 0:
                pe.wait_ge(a.v_loaded[g.slot], g.turn(16))
                pe.wait_ge(a.out_read, g.times(1, 1))
            q = g.times(steps, t * a.pairs + p)
            slot = (g.off * steps + t * a.pairs + p) % PRING
            pe.wait_ge(a.exp, q + 3)
            for half in range(2):
                j = 2 * p + half
                mm = nc.tensor.matmul(PS[w * j:w * j + w, OBANK, 0:a.nq],
                                      v_st[g.slot][0:sz, t, w * j:w * j + w],
                                      probs[0:sz, slot, half, 0:a.nq],
                                      start=(t == 0), stop=(t == a.kt - 1), tile_position=(0, w * j))
            mm.then_inc(a.used, 1)

        for x in range(a.lead):
            maxima(At(x // a.kt // 3, x // a.kt % 3), x % a.kt)
        for p in range(a.pairs):
            scores(At(0, 0), 0, p)

        def body(g):
            last = isinstance(g.loop, int) and g.loop * 3 + g.off == a.groups - 1
            for t in range(a.kt):
                for p in range(a.pairs):
                    if t + 1 < a.kt:
                        scores(g, t + 1, p)
                    elif not last:
                        scores(g.plus(1), 0, p)
                    maxima(*ahead(a, g, t), *SPREAD[a.pairs][p])
                for p in range(a.pairs):
                    values(g, t, p)
                maxima(*ahead(a, g, t), *SPREAD[a.pairs][-1])

        run_groups(pe, a, body)

    def act_attention(act, a):
        act.sem_inc(a.exp, 2)

        def body(g):
            steps = a.kt * a.pairs
            for t in range(a.kt):
                for p in range(a.pairs):
                    x = g.off * steps + t * a.pairs + p
                    q = g.times(steps, t * a.pairs + p)
                    act.wait_ge(a.pair, q + 1)
                    act.wait_ge(a.used, q + 1)
                    nc.scalar.activation(probs[0:a.size[t], x % PRING, :, 0:a.nq],
                                         PS[0:a.size[t], 2 * (x % 2):2 * (x % 2) + 2, 0:a.nq],
                                         ACT.Exp, scale=a.scale).then_inc(a.exp, 1)

        run_groups(act, a, body)

    def dve_attention(dve, a):
        steps = a.kt * a.pairs
        nch = len(a.chunks)
        dve.sem_inc(a.score_free, 3)
        dve.sem_inc(a.out_read, 1)
        dve.sem_inc(a.out_back, 1)

        def maxima(g, t, normalising=None, done=0):
            ended, items = max_step(a, g, t)
            if ended is not None:
                k = item_index(a, ended, len(a.items) - 1)[0]
                dve.wait_ge(a.score_free, 3 + k + 1)
                nc.vector.tensor_reduce(negm[0:a.qt, ended.slot, 0:a.cols],
                                        maxp[0:a.qt, ended.slot, 0:a.cols * nch].rearrange("p (c k) -> p c k", k=nch),
                                        AX.X, ALU.max, negate=True).then_inc(a.neg_ready, 1)
            for n, (i, (j, q, c)) in enumerate(items):
                k, bank = item_index(a, g, i)
                dve.wait_ge(a.score, k + 1)
                nc.vector.tensor_reduce(maxp[0:a.qt, g.slot, i:i + 1], PS[0:a.qt, SBANKS[bank], 0:a.chunks[c][1]],
                                        AX.X, ALU.max).then_inc(a.score_free, 1)
                if normalising is not None:
                    normalise(normalising, done + n)
            if ended is not None:
                k, bank = flip_index(a, ended)
                dve.wait_ge(a.score, k + 1)
                src = PS[0:a.cols, SBANKS[bank], 0:a.qt]
                nc.vector.tensor_copy(msplit[0:a.cols, ended.slot, 0, 0:a.qt], src).then_inc(a.m_high, 1)
                dve.wait_ge(a.m_high, ended.times(1, 1))
                nc.vector.tensor_tensor(msplit[0:a.cols, ended.slot, 1, 0:a.qt], src,
                                        msplit[0:a.cols, ended.slot, 0, 0:a.qt].bitcast(F32),
                                        ALU.subtract).then_inc(a.score_free, 1)
            return done + len(items) if normalising is not None else 0

        def normalise(g, part):
            view = turned[:, 0:a.nq].rearrange("p (b r) -> p b r", r=32)
            if part == 0:
                dve.wait_ge(a.used, g.times(steps, PRING + steps))
                dve.wait_ge(a.out_back, g.times(1, 1))
                nc.vector.transpose(turned[:, 0:a.nq], PS[:, OBANK, 0:a.nq]).then_inc(a.out_read, 1)
            elif part == 1:
                dve.wait_ge(a.out_read, g.times(1, 2))
                nc.vector.reciprocal(recip[:, 0:a.nq // 32], view[:, :, 31]).then_inc(a.norm, 1)
            elif part == 2:
                dve.wait_ge(a.norm, g.times(2, 1))
                nc.vector.tensor_tensor(view, view, recip[:, 0:a.nq // 32].rearrange("p (b o) -> p b o", o=1)
                                        .to_broadcast([128, a.nq // 32, 32]), ALU.mult).then_inc(a.norm, 1)
            elif part == 3:
                dve.wait_ge(a.norm, g.times(2, 2))
                dve.wait_ge(a.out_done, g.times(1, 1))
                nc.vector.transpose(back[:, 0:a.nq], turned[:, 0:a.nq]).then_inc(a.out_back, 1)

        for x in range(a.lead + a.shift):
            maxima(At(x // a.kt // 3, x // a.kt % 3), x % a.kt)

        def body(g):
            done = 0
            for t in range(a.kt):
                if t < a.kt - a.shift:
                    maxima(*ahead(a, g, t + a.shift))
                elif a.per_step > 1:
                    done = maxima(*ahead(a, g, t + a.shift), normalising=g, done=done)
                else:
                    normalise(g, done)
                    maxima(*ahead(a, g, t + a.shift))
                    normalise(g, done + 1)
                    done += 2
            for part in range(done, 4):
                normalise(g, part)

        run_groups(dve, a, body)

    def pool_outputs(pool, a):
        pool.sem_inc(a.out_done, 1)

        def body(g):
            pool.wait_ge(a.out_back, g.times(1, 2))
            nc.gpsimd.tensor_copy(a.dest[:, bass.ds(g.times(1), 1), 0:a.nq],
                                  back[:, 0:a.nq].rearrange("p (o n) -> p o n", o=1)).then_inc(a.out_done, 1)

        run_groups(pool, a, body)
        pool.wait_ge(a.out_done, 1 + a.groups)

    def pool_rows(pool, a):
        filled = a.d * len(a.terms_q)
        for s in range(3):
            m = nc.gpsimd.memset(k_st[s][96:128, :].bitcast(F32), 1.0)
        m.then_inc(a.ones, 1)
        pool.wait_ge(a.ones, 1)
        if filled < 96:
            for s in range(3):
                nc.gpsimd.memset(k_st[s][filled:96, :].bitcast(F32), 0.0)
                m = nc.gpsimd.memset(q_st[s][filled:96, :].bitcast(F32), 0.0)
            m.then_inc(a.ones, 1)
            pool.wait_ge(a.ones, 2)

    ca_prod, ca_evac = sem("ca_prod"), sem("ca_evac")
    ca_chain = sem("ca_chain")
    ca_ready = sem("ca_ready")

    def pe_ca_weights(pe):
        pe.wait_ge(first.low, first.ns)
        pe.wait_ge(first.padded, first.nv)
        for b in range(B):
            for i, w in enumerate((w_kca, w_vca)):
                for m, (f0, fn) in enumerate(FTILES):
                    for k in range(CT):
                        c0 = b * SK + SK - NCA
                        mm = nc.tensor.matmul(PS[0:fn, 6 * 0 + 2 * b + i, 4 * m:4 * m + 4], w[0:CP, k, f0:f0 + fn],
                                              ctx_t[0:CP, k, c0:c0 + NCA], start=(k == 0), stop=(k == CT - 1))
                mm.then_inc(ca_prod, 1)
        pe.wait_ge(ca_evac, 4)
        for b in range(B):
            for m, (f0, fn) in enumerate(FTILES):
                mm = nc.tensor.matmul(PS[0:32, 4 + b, 0:D], vbd[0:fn, b, m, :, :].rearrange("p h t -> p (h t)"),
                                      w_s1[0:fn, m, :], start=(m == 0), stop=(m == KF - 1))
            mm.then_inc(ca_prod, 1)

    def dve_ca_weights(dve):
        for b in range(B):
            for i, dst in enumerate((kbd, vbd)):
                dve.wait_ge(ca_prod, 2 * b + i + 1)
                for m, (f0, fn) in enumerate(FTILES):
                    o = nc.vector.tensor_tensor(dst[0:fn, b, m, :, :],
                                                hmask[0:fn, m, :].rearrange("p (h t) -> p h t", t=NCA),
                                                PS[0:fn, 2 * b + i, 4 * m:4 * m + 4].rearrange(
                                                    "p (o t) -> p o t", o=1).to_broadcast([fn, H0, NCA]), ALU.mult)
                o.then_inc(ca_evac, 1)
        for b in range(B):
            dve.wait_ge(ca_prod, 4 + b + 1)
            nc.vector.tensor_copy(vw[:, b, :], PS[0:32, 4 + b, 0:D]).then_inc(ca_evac, 1)

    def pe_ca_tail(pe):
        for b in range(B):
            pe.wait_ge(A_CA.out_done, 1 + A_CA.groups)
            if b:
                pe.wait_ge(ca_ready, 5 * b)
            for m, (f0, fn) in enumerate(FTILES):
                for g in range(4):
                    mm = nc.tensor.matmul(PS[0:fn, m, 0:UQ], w_pad_b[:, g, f0:f0 + fn], ca_t[:, b * 4 + g, :],
                                          start=(g == 0), stop=(g == 3))
                mm.then_inc(ca_prod, 1)
            pe.wait_ge(ca_ready, 5 * b + 3)
            for h in range(2):
                for m, (f0, fn) in enumerate(FTILES):
                    mm = nc.tensor.matmul(PS[0:CP, 3, 32 * h:32 * h + 32], q2t[0:fn, m, 96 * h:96 * h + 96],
                                          kbd[0:fn, b, m, :, :].rearrange("p h t -> p (h t)"),
                                          start=(m == 0), stop=(m == KF - 1))
            mm.then_inc(ca_prod, 1)
            pe.wait_ge(ca_evac, 6 + 2 * b + 2)
            for h in range(2):
                mm = nc.tensor.matmul(PS[0:32, 4, 0:SQ], p3[:, b, h, :], onehot[:, h, :],
                                      start=(h == 0), stop=(h == 1))
            mm.then_inc(ca_prod, 1)

    def act_ca_tail(act):
        for b in range(B):
            for m, (f0, fn) in enumerate(FTILES):
                act.wait_ge(ca_prod, 6 + 5 * b + m + 1)
                nc.scalar.copy(q2t[0:fn, m, :], PS[0:fn, m, 0:UQ]).then_inc(ca_ready, 1)
            act.wait_ge(ca_evac, 6 + 2 * b + 1)
            nc.scalar.activation(p3[:, b, :, :], s3[:, :, :], ACT.Exp, scale=A_CA.scale).then_inc(ca_ready, 1)
            act.wait_ge(ca_prod, 6 + 5 * b + 5)
            nc.scalar.copy(ep3[:, b, :], PS[0:32, 4, 0:SQ]).then_inc(ca_ready, 1)

    def dve_ca_tail(dve):
        for b in range(B):
            dve.wait_ge(ca_prod, 6 + 5 * b + 4)
            view = "p h (g t) -> p (h g) t"
            s_in = PS[0:CP, 3, 0:64].rearrange("p (g t) -> p g t", t=NCA)
            m16 = recip[0:CP, 0:16]
            nc.vector.tensor_reduce(m16, s_in, AX.X, ALU.max).then_inc(ca_chain, 1)
            dve.wait_ge(ca_chain, 3 * b + 1)
            nc.vector.tensor_tensor(s3[:, :, :].rearrange(view, t=NCA), s_in,
                                    m16.rearrange("p (g o) -> p g o", o=1).to_broadcast([CP, 16, NCA]),
                                    ALU.subtract).then_inc(ca_evac, 1)
            dve.wait_ge(ca_ready, 5 * b + 4)
            e = p3[:, b, :, :].rearrange(view, t=NCA)
            nc.vector.tensor_reduce(recip[0:CP, 16:32], e, AX.X, ALU.add).then_inc(ca_chain, 1)
            dve.wait_ge(ca_chain, 3 * b + 2)
            nc.vector.reciprocal(recip[0:CP, 0:16], recip[0:CP, 16:32]).then_inc(ca_chain, 1)
            dve.wait_ge(ca_chain, 3 * b + 3)
            nc.vector.tensor_tensor(e, e, recip[0:CP, 0:16].rearrange("p (g o) -> p g o", o=1)
                                    .to_broadcast([CP, 16, NCA]), ALU.mult).then_inc(ca_evac, 1)

    class Join:

        def __init__(self, name, groups, w, bias, norm, ca):
            self.name, self.groups, self.w, self.bias, self.norm, self.ca = name, groups, w, bias, norm, ca
            self.biased = sem(name + "_biased")
            self.product = sem(name + "_product")
            self.added = sem(name + "_added")
            self.chain = sem(name + "_chain")
            self.root = sem(name + "_root")
            self.normed = sem(name + "_normed")
            self.flipped = sem(name + "_flipped")
            self.ready = sem(name + "_ready")

    join0 = Join("join0", 4, w_pad_a, 0, 0, True)
    join1 = Join("join1", 5, w_pad_b, 1, 1, False)
    join2 = Join("join2", 5, w_pad_a, 2, 2, False)

    def pool_bias(pool, jn):
        for t in range(TT):
            o = nc.gpsimd.tensor_tensor(resid[:, t, :], resid[:, t, :], brows[:, jn.bias, :], ALU.add)
        o.then_inc(jn.biased, 1)

    def pe_join(pe, jn, a):
        pe.wait_ge(a.out_done, 1 + a.groups)
        if jn.ca:
            pe.wait_ge(ca_ready, 10)

        def product(t):
            b, c = t // 4, (t % 4) * 128
            if t >= 4:
                pe.wait_ge(jn.added, t - 3)
            for g in range(jn.groups):
                mm = nc.tensor.matmul(PS[:, t % 4, 0:D], out_t[:, b * jn.groups + g, c:c + 128], jn.w[:, g, :],
                                      start=(g == 0), stop=(g == jn.groups - 1 and not jn.ca))
            if jn.ca:
                mm = nc.tensor.matmul(PS[:, t % 4, 0:D], ep3[:, b, c:c + 128], vw[:, b, :], start=False, stop=True)
            mm.then_inc(jn.product, 1)

        def flip(t):
            pe.wait_ge(jn.normed, t + 1)
            if t >= 4:
                pe.wait_ge(jn.ready, t - 3)
            for m, (f0, fn) in enumerate(FTILES):
                mm = nc.tensor.transpose(PS[0:fn, 4 + t % 4, 128 * m:128 * m + 128], xhat[:, t % 2, f0:f0 + fn],
                                         ident[:, :])
            mm.then_inc(jn.flipped, 1)

        for t in range(TT + 2):
            if t < TT:
                product(t)
            if t >= 2:
                flip(t - 2)

    def dve_join(dve, jn):
        dve.wait_ge(jn.biased, 1)
        for t in range(TT):
            dve.wait_ge(jn.product, t + 1)
            nc.vector.tensor_tensor(resid[:, t, :], PS[:, t % 4, 0:D], resid[:, t, :], ALU.add).then_inc(jn.added, 1)
            dve.wait_ge(jn.added, t + 1)
            nc.vector.bn_stats(stats[:, :], resid[:, t, :]).then_inc(jn.chain, 1)
            dve.wait_ge(jn.chain, 3 * t + 1)
            nc.vector.bn_aggr(mv[:, t, :], stats[:, :]).then_inc(jn.chain, 1)
            dve.wait_ge(jn.chain, 3 * t + 2)
            dve.wait_ge(jn.root, t + 1)
            nc.vector.reciprocal(rstd[:, t:t + 1], std[:, t:t + 1]).then_inc(jn.chain, 1)
            dve.wait_ge(jn.chain, 3 * t + 3)
            if t >= 2:
                dve.wait_ge(jn.flipped, t - 1)
            nc.vector.tensor_scalar(xhat[:, t % 2, :], resid[:, t, :], mv[:, t, 0:1], rstd[:, t:t + 1],
                                    ALU.subtract, ALU.mult).then_inc(jn.normed, 1)

    def act_join(act, jn):
        def flipped(t):
            act.wait_ge(jn.flipped, t + 1)
            for m, (f0, fn) in enumerate(FTILES):
                c = 6 * jn.norm + m
                o = nc.scalar.activation(act_t[0:fn, m, t * 128:(t + 1) * 128],
                                         PS[0:fn, 4 + t % 4, 128 * m:128 * m + 128], ACT.Identity,
                                         bias=params[0:fn, c + 3:c + 4], scale=params[0:fn, c:c + 1])
            o.then_inc(jn.ready, 1)

        for t in range(TT + 1):
            if t < TT:
                act.wait_ge(jn.chain, 3 * t + 2)
                nc.scalar.activation(std[:, t:t + 1], mv[:, t, 1:2], ACT.Sqrt, bias=eps[:, :]).then_inc(jn.root, 1)
            if t:
                flipped(t - 1)

    ff_loaded, ff_product, ff_gelu, ff_inner = sem("ff_loaded"), sem("ff_product"), sem("ff_gelu"), sem("ff_inner")
    ff_biased, ff_down, ff_out, out_stored = sem("ff_biased"), sem("ff_down"), sem("ff_out"), sem("out_stored")

    def pe_ff(pe):
        pe.wait_ge(join2.ready, TT)
        pe.wait_ge(ff_loaded, 32)
        for half in range(B):
            for m in range(FT):
                i = half * FT + m
                if i >= 2:
                    pe.wait_ge(ff_inner, i - 1)
                for part in range(2):
                    f0 = part * FF + m * 128
                    for k, p in enumerate(XP):
                        mm = nc.tensor.matmul(PS[:, 2 * (i % 2) + part, :], w_ff1[0:p, k, f0:f0 + 128],
                                              act_t[0:p, k, half * SQ:(half + 1) * SQ], start=(k == 0), stop=(k == 2))
                mm.then_inc(ff_product, 1)
        for t in range(TT):
            pe.wait_ge(ff_inner, FT * (t // 4 + 1))
            if t >= 4:
                pe.wait_ge(ff_out, t - 3)
            for m in range(FT):
                mm = nc.tensor.matmul(PS[:, 4 + t % 4, 0:D], ff_t[:, m, t * 128:(t + 1) * 128], w_ff2[:, m, :],
                                      start=(m == 0), stop=(m == FT - 1))
            mm.then_inc(ff_down, 1)

    def act_ff(act):
        for i in range(B * FT):
            act.wait_ge(ff_product, i + 1)
            if i >= 2:
                act.wait_ge(ff_inner, i - 1)
            c = 18 + FT + i % FT
            nc.scalar.activation(gelu[:, i % 2, :], PS[:, 2 * (i % 2) + 1, :], ACT.Gelu,
                                 bias=params[:, c:c + 1]).then_inc(ff_gelu, 1)

    def dve_ff(dve):
        for i in range(B * FT):
            m, half = i % FT, i // FT
            dve.wait_ge(ff_gelu, i + 1)
            nc.vector.scalar_tensor_tensor(out=ff_t[:, m, half * SQ:(half + 1) * SQ], in0=PS[:, 2 * (i % 2), :],
                                           scalar=params[:, 18 + m:19 + m], in1=gelu[:, i % 2, :],
                                           op0=ALU.add, op1=ALU.mult).then_inc(ff_inner, 1)
        dve.wait_ge(ff_biased, 1)
        for t in range(TT):
            dve.wait_ge(ff_down, t + 1)
            nc.vector.tensor_tensor(resid[:, t, :], PS[:, 4 + t % 4, 0:D], resid[:, t, :], ALU.add).then_inc(ff_out, 1)

    pads_zero, pads_set = sem("pads_zero"), sem("pads_set")
    block = nc.Block()
    with block:

        @block.sync
        def _(sp):
            for dst, name in loads["a"]:
                sp.dma_start(dst[:], ins[name]).then_inc(loaded_a, 16)
            for dst, name in loads["c"]:
                sp.dma_start(dst[:], ins[name]).then_inc(loaded_c, 16)
            for dst, name in loads["b"]:
                sp.dma_start(dst[:], ins[name]).then_inc(loaded_b, 16)
            sp.dma_start(brows[:].rearrange("p a d -> p (a d)"), ins["brows"].partition_broadcast(128)).then_inc(loaded_b, 16)
            sp_projection(sp, first)
            sp_attention(sp, A_MAIN, first, None)
            sp.wait_ge(ca_evac, 6)
            for dst, name in ((w_s0, "q1"), (w_s1, "k1")):
                sp.dma_start(dst[:], ins[name]).then_inc(loaded_b, 16)
            sp_attention(sp, A_CA, first, A_MAIN)
            sp.wait_ge(ca_prod, 6 + 10)
            sp.dma_start(w_pad_b[:], ins["o1_g"]).then_inc(loaded_b, 16)
            sp.wait_ge(join0.product, TT)
            sp.dma_start(w_pad_a[:], ins["o2_g"]).then_inc(loaded_b, 16)
            sp_projection(sp, selfp)
            sp.wait_ge(selfp.padded, selfp.nv)
            sp.dma_start(w_s0[:], ins["q2"]).then_inc(loaded_b, 16)
            sp_attention(sp, A_SELF, selfp, A_CA)
            sp_projection(sp, crossp)
            sp_attention(sp, A_CROSS, crossp, A_SELF)
            sp.wait_ge(A_CROSS.out_done, 1 + A_CROSS.groups)
            sp.dma_start(w_ff1[:], ins["ff_w1"]).then_inc(ff_loaded, 16)
            sp.dma_start(w_ff2[:], ins["ff_w2"]).then_inc(ff_loaded, 16)
            for t in range(TT):
                sp.wait_ge(ff_out, t + 1)
                sp.dma_start(out_dram[t * 128:(t + 1) * 128, :], resid[:, t, :]).then_inc(out_stored, 16)
            sp.wait_ge(out_stored, 16 * TT)

        @block.tensor
        def _(pe):
            pe.wait_ge(loaded_a, ALL_A)
            pe_projection(pe, first)
            pe_ca_weights(pe)
            pe.wait_ge(ca_evac, 6)
            pe_attention(pe, A_MAIN)
            pe.wait_ge(A_MAIN.out_read, 1 + A_MAIN.groups)
            pe_attention(pe, A_CA)
            pe_ca_tail(pe)
            pe_join(pe, join0, A_MAIN)
            pe.wait_ge(loaded_b, ALL_B + 16 * 4)
            pe.wait_ge(join0.ready, TT)
            pe_projection(pe, selfp)
            pe.wait_ge(selfp.low, selfp.ns)
            pe.wait_ge(selfp.padded, selfp.nv)
            pe_attention(pe, A_SELF)
            pe_join(pe, join1, A_SELF)
            pe.wait_ge(loaded_b, ALL_B + 16 * 5)
            pe.wait_ge(join1.ready, TT)
            pe_projection(pe, crossp)
            pe.wait_ge(crossp.low, crossp.ns)
            pe_attention(pe, A_CROSS)
            pe_join(pe, join2, A_CROSS)
            pe_ff(pe)

        @block.scalar
        def _(act):
            act.wait_ge(loaded_a, ALL_A)
            act.wait_ge(pads_set, 1)
            act_projection(act, first)
            act.wait_ge(loaded_b, ALL_B)
            act_attention(act, A_MAIN)
            act_attention(act, A_CA)
            act_ca_tail(act)
            act_join(act, join0)
            act_projection(act, selfp)
            act_attention(act, A_SELF)
            act_join(act, join1)
            act_projection(act, crossp)
            act_attention(act, A_CROSS)
            act_join(act, join2)
            act_ff(act)

        @block.vector
        def _(dve):
            dve.wait_ge(loaded_a, ALL_A)
            dve_projection(dve, first)
            dve.wait_ge(loaded_b, ALL_B)
            dve_ca_weights(dve)
            dve_attention(dve, A_MAIN)
            dve_attention(dve, A_CA)
            dve_ca_tail(dve)
            dve_join(dve, join0)
            dve_projection(dve, selfp)
            dve_attention(dve, A_SELF)
            dve_join(dve, join1)
            dve_projection(dve, crossp)
            dve_attention(dve, A_CROSS)
            dve_join(dve, join2)
            dve_ff(dve)

        @block.gpsimd
        def _(pool):
            nc.gpsimd.memset(eps[:], EPS)
            nc.gpsimd.memset(vpad0[:], 0.0)
            nc.gpsimd.memset(vpad1[:], 0.0).then_inc(pads_zero, 1)
            pool.wait_ge(pads_zero, 1)
            nc.gpsimd.memset(vpad0[:, :, :, 31:32], 1.0)
            nc.gpsimd.memset(vpad0[:, :, :, 63:64], 1.0)
            nc.gpsimd.memset(vpad1[:, :, :, 31:32], 1.0).then_inc(pads_set, 1)
            pool.wait_ge(pads_set, 1)
            pool_rows(pool, A_MAIN)
            pool.wait_ge(first.padded, first.nv)
            pool.wait_ge(loaded_b, ALL_B)
            pool_bias(pool, join0)
            pool_outputs(pool, A_MAIN)
            pool_outputs(pool, A_CA)
            pool.wait_ge(A_CA.pair, A_CA.groups * A_CA.kt * A_CA.pairs)
            pool_rows(pool, A_SELF)
            pool.wait_ge(join0.normed, TT)
            pool_bias(pool, join1)
            pool_outputs(pool, A_SELF)
            pool.wait_ge(join1.normed, TT)
            pool_bias(pool, join2)
            pool_outputs(pool, A_CROSS)
            pool.wait_ge(join2.normed, TT)
            for t in range(TT):
                o = nc.gpsimd.tensor_tensor(resid[:, t, :], resid[:, t, :], brows[:, 3, :], ALU.add)
            o.then_inc(ff_biased, 1)


def kernel(**inputs):
    import numpy as _np
    import concourse.bacc as _bacc
    from concourse import mybir as _mybir
    from concourse.bass_utils import run_bass_kernel_spmd as _run

    i = {k: _np.asarray(v) for k, v in inputs.items()}

    def tiles(a, p=128):
        n = -(-a.shape[0] // p)
        full = _np.zeros((n * p, a.shape[1]), a.dtype)
        full[:a.shape[0]] = a
        return full.reshape(n, p, a.shape[1]).transpose(1, 0, 2)

    def by_group(w, heads, d, width):
        g = 128 // width
        full = _np.zeros((heads // g, 128, w.shape[1]), w.dtype)
        for h in range(heads):
            r = width * (h % g)
            full[h // g, r:r + min(d, 31)] = w[h * d:h * d + min(d, 31)]
            if d > 31:
                full[h // g, r + 32:r + 32 + d - 31] = w[h * d + 31:(h + 1) * d]
        if heads // g < 5:
            full = _np.concatenate([full, _np.zeros((5 - heads // g, 128, w.shape[1]), w.dtype)])
        return full.transpose(1, 0, 2)

    x = i["x"].reshape(TOK, D)
    ctx = i["ctx_768"].reshape(B * SK, DC)
    L0, L1 = "L0_xattn_", "L1_xattn_"
    f32 = x.dtype
    one = _np.zeros((UQ, SQ), f32)
    one[_np.linspace(0, DC - 1, SQ).astype(_np.int64), _np.arange(SQ)] = 1.0
    mask = _np.zeros((D, H0, NCA), f32)
    for h in range(H0):
        mask[h * D0:(h + 1) * D0, h] = 1.0
    cols = [tiles(i[L1 + n][:, None])[:, :, 0] for n in ("n1_g", "n1_b", "n2_g", "n2_b", "n3_g", "n3_b", "ff_b1")]
    feed = {
        "x_t": tiles(x.T), "x": tiles(x), "ctx_t": tiles(ctx.T, CP),
        "ca": i["ctx_768"][:, SK - NCA:].transpose(1, 0, 2),
        "Wq": tiles(i[L0 + "Wq"]), "Wout": tiles(i[L0 + "Wout"]),
        "Wk": tiles(i[L0 + "Wk"], CP), "Wv": tiles(i[L0 + "Wv"], CP),
        "Wk_ca": tiles(i[L0 + "Wk_ca"], CP), "Wv_ca": tiles(i[L0 + "Wv_ca"], CP), "Wq_ca": i[L0 + "Wq_ca"],
        "Wq_g": by_group(i[L0 + "Wq"], H0, D0, 64), "Wout_g": by_group(i[L0 + "Wout"], H0, D0, 64),
        "q1": tiles(i[L1 + "q1"]), "k1": tiles(i[L1 + "k1"]), "v1": tiles(i[L1 + "v1"]), "q2": tiles(i[L1 + "q2"]),
        "k2": tiles(i[L1 + "k2"], CP), "v2": tiles(i[L1 + "v2"], CP),
        "o1_g": by_group(i[L1 + "o1_w"], H1, D1, 32), "o2_g": by_group(i[L1 + "o2_w"], H1, D1, 32),
        "ff_w1": tiles(i[L1 + "ff_w1"]), "ff_w2": tiles(i[L1 + "ff_w2"]),
        "params": _np.concatenate(cols, axis=1),
        "brows": _np.concatenate([i[L0 + "b_out"], i[L1 + "o1_b"], i[L1 + "o2_b"], i[L1 + "ff_b2"]]),
        "onehot": tiles(one, CP), "hmask": tiles(mask.reshape(D, H0 * NCA)), "ident": _np.eye(128, dtype=f32),
    }
    nc = _bacc.Bacc("TRN2", target_bir_lowering=False, num_devices=1)
    arrays, args = {}, {}
    for name, a in feed.items():
        a = _np.ascontiguousarray(a)
        arrays[f"in_{name}"] = a
        args[name] = nc.dram_tensor(f"in_{name}", a.shape, _mybir.dt.from_np(a.dtype), kind="ExternalInput").ap()
    out = nc.dram_tensor("out_0", (TOK, D), _mybir.dt.float32, kind="ExternalOutput").ap()
    build(nc, args, out)
    r = _run(nc, [arrays], core_ids=[0])
    return r.results[0]["out_0"].reshape(B, SQ, D)
```

```python
import numpy as np
import concourse.bass as bass
from concourse import mybir

F32 = mybir.dt.float32
F32R = mybir.dt.float32r
ALU = mybir.AluOpType
ACT = mybir.ActivationFunctionType
AX = mybir.AxisListType

B, SQ, D = 2, 512, 320
SK, DC = 1024, 192
TOK = B * SQ
TT = TOK // 128
FTILES = [(0, 128), (128, 128), (256, 64)]
KF = len(FTILES)
CT, CP = 2, 96
NCA = 4
UQ = DC
H0, D0 = 8, 40
H1, D1 = 20, 16
FF = 4 * D
FT = FF // 128
EPS = 1e-5
RING = 4
VRING = (4, 3)
PRING = 4
SBANKS = (4, 5, 6)
SPREAD = {1: ((0, 3), (3, 4)), 2: ((0, 1), (1, 3), (3, 4))}
OBANK = 7


class Attention:

    def __init__(self, name, heads, d, width, terms_q, terms_k, nq, qt, keys, lead):
        self.name, self.heads, self.d = name, heads, d
        self.width = width
        self.g = 128 // width
        self.pairs = self.g // 2
        self.groups = B * heads // self.g
        self.terms_q, self.terms_k = terms_q, terms_k
        self.rows = max(96, d * len(terms_q))
        self.nq, self.qt, self.nqt = nq, qt, nq // qt
        self.keys = keys
        self.kt = -(-keys // 128)
        self.size = [min(128, keys - 128 * t) for t in range(self.kt)]
        self.chunks = [(c, min(512, keys - c)) for c in range(0, keys, 512)]
        self.items = [(j, q, c) for j in range(self.g) for q in range(self.nqt) for c in range(len(self.chunks))]
        self.per_step = len(self.items) // self.kt
        self.lead = lead
        self.cols = self.g * self.nqt
        self.scale = float(d) ** -0.5
        self.shift = 1
        span = (lead + self.shift + self.kt - 1) // self.kt
        self.loops = (self.groups - span) // 3
        assert self.kt < lead < 2 * self.kt + 1 and len(self.items) % self.kt == 0


HH_L = (0, 0, 1)
H_LH = (0, 1, 0)
HHLL = (0, 0, 1, 1)
HLHL = (0, 1, 0, 1)
A_MAIN = Attention("main", H0, D0, 64, HH_L, H_LH, SQ, 128, SK - NCA, 13)
A_CA = Attention("ca", H0, D0, 64, HH_L, H_LH, UQ, 96, SQ, 8)
A_SELF = Attention("self", H1, D1, 32, HHLL, HLHL, SQ, 128, SQ, 7)
A_CROSS = Attention("cross", H1, D1, 32, HHLL, HLHL, SQ, 128, SK, 12)


class At:

    def __init__(self, loop, off):
        self.loop, self.off = loop, off
        self.slot = off % 3

    def plus(self, k):
        return At(self.loop, self.off + k)

    def times(self, per, k=0):
        return self.loop * (3 * per) + (self.off * per + k)

    def turn(self, per, k=0):
        return self.loop * per + ((self.off // 3 + 1) * per + k)


def build(nc, ins, out_dram):
    at = [16512]

    def place(name, shape, dt=F32, offset=None):
        size = int(np.prod(shape[1:])) * 4
        if offset is None:
            offset = at[0]
            at[0] += -(-size // 32) * 32
        return nc.alloc_sbuf_tensor_at(name, shape, dt, offset=offset)

    def region(size):
        start = at[0]
        at[0] += size
        return start

    ident = place("ident", [128, 128])
    params = place("params", [128, 38])
    brows = place("brows", [128, 4, D])
    onehot = place("onehot", [CP, 2, SQ])
    hmask = place("hmask", [128, KF, H0 * NCA])
    first_weight = at[0]
    w_s0 = place("w_s0", [128, KF, D])
    w_s1 = place("w_s1", [128, KF, D])
    w_s2 = place("w_s2", [128, KF, D])
    w_pad_b = place("w_pad_b", [128, 5, D])
    w_pad_a = place("w_pad_a", [128, 5, D])
    act_high = place("act_high", [128, KF, TOK], F32R, offset=first_weight)
    act_low = place("act_low", [128, KF, TOK], F32R, offset=at[0])
    act_t = place("act_t", [128, KF, TOK])
    resid = place("resid", [128, TT, D])
    r1 = region(max(16384 + 4 * 2560 + 2 * 2560, 20480 + 6144))
    xpad = place("xpad", [128, 2, H0, 64], offset=r1 + 16384)
    ctx_t = place("ctx_t", [CP, CT, B * SK], offset=r1)
    w_k0 = place("w_k0", [CP, CT, D], offset=r1 + 16384)
    w_v0 = place("w_v0", [CP, CT, D], offset=r1 + 18944)
    w_k2 = place("w_k2", [CP, CT, D], offset=r1 + 21504)
    w_v2 = place("w_v2", [CP, CT, D], offset=r1 + 24064)
    w_kca = place("w_kca", [CP, CT, D], offset=r1 + 26624)
    w_vca = place("w_vca", [CP, CT, D], offset=r1 + 29184)
    out_t = place("out_t", [128, 10, SQ], offset=r1)
    ca_t = place("ca_t", [128, 8, UQ], offset=r1 + 20480)
    r2 = region(3 * 8192 + 3 * 16384 + 3 * 4096 + PRING * 4096)
    q_st = [place(f"q_st{s}", [128, 2048], F32R, offset=r2 + 8192 * s) for s in range(3)]
    k_st = [place(f"k_st{s}", [128, 4096], F32R, offset=r2 + 24576 + 16384 * s) for s in range(3)]
    v_st = [place(f"v_st{s}", [128, 8, 128], F32, offset=r2 + 73728 + 4096 * s) for s in range(3)]
    probs = place("probs", [128, PRING, 2, SQ], F32, offset=r2 + 86016)
    w1_raw = place("w1_raw", [128, KF, 2 * FF], F32, offset=r2)
    ff_raw = place("ff_raw", [128, FT, SQ], F32, offset=r2 + 61440)
    w2_raw = place("w2_raw", [128, FT, D], F32, offset=r1)
    w1_low = place("w1_low", [128, KF, 2 * FF], F32R, offset=r2)
    w1_high = place("w1_high", [128, KF, 2 * FF], F32R, offset=r2 + 30720)
    ff_low = place("ff_low", [128, FT, SQ], F32R, offset=r2 + 61440)
    ff_high = place("ff_high", [128, FT, SQ], F32R, offset=r2 + 81920)
    w2_low = place("w2_low", [128, FT, D], F32R, offset=r1)
    w2_high = place("w2_high", [128, FT, D], F32R, offset=r1 + 12800)
    gelu = place("gelu", [128, 2, SQ], F32, offset=r1 + 25600)
    split = place("split", [128, RING, 2, SQ], F32R, offset=r2 + 86016)
    vpad0 = place("vpad0", [128, VRING[0], H0, 64], offset=r2 + 73728)
    ep3 = place("ep3", [32, B, SQ], offset=r2 + 73728)
    vpad1 = place("vpad1", [128, VRING[1], H1, 32])
    maxp = place("maxp", [128, 3, 32])
    negm = place("negm", [128, 3, 16])
    msplit = place("msplit", [16, 3, 2, 128], F32R)
    r5 = region(2048)
    turned = place("turned", [128, SQ], offset=r5)
    back = place("back", [128, SQ])
    recip = place("recip", [128, 32])
    ca_nat = place("ca_nat", [NCA, B, DC], offset=r5)
    r6 = region(2560)
    xhat = place("xhat", [128, 2, D], offset=r6)
    wqca = place("wqca", [NCA, D], offset=r6)
    q2t = place("q2t", [128, KF, UQ], offset=r6)
    stats = place("stats", [128, 6])
    mv = place("mv", [128, TT, 2])
    rstd = place("rstd", [128, TT])
    std = place("std", [128, TT])
    eps = place("eps", [128, 1])
    kbd = place("kbd", [128, B, KF, H0, NCA])
    vbd = place("vbd", [128, B, KF, H0, NCA])
    vw = place("vw", [32, B, D], offset=r1 + 26624)
    p3 = place("p3", [CP, B, 2, 32], offset=r1 + 29184)
    s3 = place("s3", [CP, 2, 32], offset=r1 + 29696)
    assert at[0] <= 229344, at[0]
    PS = nc.alloc_psum_tensor("PS", [128, 8, 512], F32)

    def dram(name, shape):
        return nc.dram_tensor(name, shape, F32, kind="Internal").ap()

    q0_d, x0_d = dram("q0_d", [2, B * D, SQ]), dram("x0_d", [2, B * D, SQ])
    k0_d, cq_d = dram("k0_d", [2, B * D, SK]), dram("cq_d", [2, B * D, UQ])
    q1_d, k1_d = dram("q1_d", [2, B * D, SQ]), dram("k1_d", [2, B * D, SQ])
    q2_d, k2_d = dram("q2_d", [2, B * D, SQ]), dram("k2_d", [2, B * D, SK])
    v0_d, vx_d = dram("v0_d", [8, 128, 8, 128]), dram("vx_d", [8, 128, 4, 128])
    v1_d, v2_d = dram("v1_d", [10, 128, 4, 128]), dram("v2_d", [10, 128, 8, 128])

    count = [0]

    def sem(name):
        count[0] += 1
        return nc.alloc_semaphore(name)

    loads = {
        "a": [(act_t, "x_t"), (w_s0, "Wq")],
        "c": [(ctx_t, "ctx_t"), (w_k0, "Wk"), (wqca, "Wq_ca"), (ca_nat, "ca"), (w_v0, "Wv")],
        "x": [(resid, "x")],
        "b": [(w_k2, "k2"), (w_v2, "v2"), (w_kca, "Wk_ca"), (w_vca, "Wv_ca"), (w_s1, "Wout"),
              (hmask, "hmask"), (ident, "ident"), (onehot, "onehot"),
              (params, "params"), (w_pad_a, "Wout_g"), (w_pad_b, "Wq_g"), (w_s2, "v1")],
    }
    loaded_x = sem("loaded_x")
    loaded_a, loaded_c, loaded_b = sem("loaded_a"), sem("loaded_c"), sem("loaded_b")
    ALL_A, ALL_C, ALL_B = 16 * len(loads["a"]), 16 * len(loads["c"]), 16 * (len(loads["b"]) + 1)

    def rows_of(dst, b, m, c, n):
        f0, fn = FTILES[m]
        return dst[:, b * D + f0:b * D + f0 + fn, c:c + n].rearrange("t f n -> f t n")

    def feat_job(w, parts, ktiles, src, m, b, c, n, dst):
        f0, fn = FTILES[m]
        return dict(kind="s", mm=[(w[0:p, k, f0:f0 + fn], src(k, p)) for k, p in zip(range(ktiles), parts)],
                    m=fn, n=n, src=None, dst=rows_of(dst, b, m, c, n))

    XP = [128, 128, 64]
    CPS = [CP, CP]

    def x_cols(b):
        return lambda k, p: act_t[0:p, k, b * SQ:(b + 1) * SQ]

    def c_cols(b, c):
        return lambda k, p: ctx_t[0:p, k, b * SK + c:b * SK + c + 512]

    def v_job(mm, layer, dst, b, t):
        return dict(kind="v", mm=mm, layer=layer, src=None,
                    dst=dst[b * (4 if layer == 0 else 5):(b + 1) * (4 if layer == 0 else 5), :, t, :]
                    .rearrange("g p c -> p g c"))

    C_FROM = 2 * B * KF

    def first_jobs():
        jobs = []
        for b in range(B):
            jobs += [feat_job(w_s0, XP, KF, x_cols(b), m, b, 0, SQ, q0_d) for m in range(KF)]
            jobs += [dict(kind="s", mm=None, m=FTILES[m][1], n=SQ, src=x_cols(b)(m, FTILES[m][1]),
                          dst=rows_of(x0_d, b, m, 0, SQ)) for m in range(KF)]
        for b in range(B):
            for c in (0, 512):
                jobs += [feat_job(w_k0, CPS, CT, c_cols(b, c), m, b, c, 512, k0_d) for m in range(KF)]
            jobs += [dict(kind="s", mm=[(wqca[:, FTILES[m][0]:FTILES[m][0] + FTILES[m][1]], ca_nat[:, b, :])],
                          m=FTILES[m][1], n=UQ, src=None, dst=rows_of(cq_d, b, m, 0, UQ)) for m in range(KF)]
            for t in range(8):
                jobs.append(v_job([(ctx_t[0:CP, k, b * SK + t * 128:b * SK + t * 128 + 128], w_v0[0:CP, k, :])
                                   for k in range(CT)], 0, v0_d, b, t))
        return jobs

    def second_jobs():
        jobs = []
        for b in range(B):
            for c in (0, 512):
                jobs += [feat_job(w_k2, CPS, CT, c_cols(b, c), m, b, c, 512, k2_d) for m in range(KF)]
            for t in range(8):
                jobs.append(v_job([(ctx_t[0:CP, k, b * SK + t * 128:b * SK + t * 128 + 128], w_v2[0:CP, k, :])
                                   for k in range(CT)], 1, v2_d, b, t))
        return jobs

    def self_jobs():
        jobs = []
        for b in range(B):
            for m in range(KF):
                jobs.append(feat_job(w_s0, XP, KF, x_cols(b), m, b, 0, SQ, q1_d))
                jobs.append(feat_job(w_s1, XP, KF, x_cols(b), m, b, 0, SQ, k1_d))
            for t in range(4):
                jobs.append(v_job([(act_t[0:p, k, (b * 4 + t) * 128:(b * 4 + t + 1) * 128], w_s2[0:p, k, :])
                                   for k, p in enumerate(XP)], 1, v1_d, b, t))
        return jobs

    def cross_jobs():
        return [feat_job(w_s0, XP, KF, x_cols(b), m, b, 0, SQ, q2_d) for b in range(B) for m in range(KF)]

    class Projection:
        def __init__(self, name, jobs, banks=(0, 1, 2, 3), vbanks=(4, 5)):
            self.banks, self.vbanks = banks, vbanks
            self.jobs, ns, nv, nm = [], 0, 0, 0
            for at_, j in enumerate(jobs):
                j["at"] = at_
                if j["kind"] == "s":
                    j["i"], ns = ns, ns + 1
                    if j["mm"]:
                        nm += 1
                        j["mm_count"] = nm
                else:
                    j["i"], nv = nv, nv + 1
                    if j["mm"]:
                        nm += 1
                        j["mm_count"] = nm
                self.jobs.append(j)
            self.ns, self.nv = ns, nv
            self.product = sem(name + "_product")
            self.high = sem(name + "_high")
            self.low = sem(name + "_low")
            self.padded = sem(name + "_padded") if nv else None
            self.stored = [sem(f"{name}_stored{s}") for s in range(RING)]
            self.vring = VRING[jobs[-1].get("layer", 0)]
            self.vstored = [sem(f"{name}_vstored{s}") for s in range(self.vring if nv else 0)]

        def wait_stored(self, eng):
            for s in range(RING):
                n = len(range(s, self.ns, RING))
                if n:
                    eng.wait_ge(self.stored[s], 16 * n)

        def wait_vstored(self, eng):
            for s in range(self.vring if self.nv else 0):
                eng.wait_ge(self.vstored[s], 16 * len(range(s, self.nv, self.vring)))

    first = Projection("first", first_jobs())
    second = Projection("second", second_jobs(), (0, 1, 2), (3, OBANK))
    selfp = Projection("selfp", self_jobs())
    crossp = Projection("crossp", cross_jobs())

    def share(ph, x, of):
        n = len(ph.jobs)
        return ph.jobs[x * n // of:(x + 1) * n // of]

    def split_bank(ph, j):
        return PS[0:j["m"], ph.banks[j["i"] % len(ph.banks)], 0:j["n"]]

    def value_bank(ph, j):
        return PS[:, ph.vbanks[j["i"] % 2], 0:D]

    def inputs_in(eng, ph, j):
        if ph is first and j["at"] == C_FROM:
            eng.wait_ge(loaded_c, ALL_C)

    def pe_projection(pe, ph, jobs=None):
        nb = len(ph.banks)
        for j in ph.jobs if jobs is None else jobs:
            inputs_in(pe, ph, j)
            if not j["mm"]:
                continue
            if j["kind"] == "s":
                if j["i"] >= nb:
                    pe.wait_ge(ph.low, j["i"] - nb + 1)
                o = split_bank(ph, j)
            else:
                if j["i"] >= 2:
                    pe.wait_ge(ph.padded, j["i"] - 2 + 1)
                o = value_bank(ph, j)
            for k, (w, a) in enumerate(j["mm"]):
                mm = nc.tensor.matmul(o, w, a, start=(k == 0), stop=(k == len(j["mm"]) - 1))
            mm.then_inc(ph.product, 1)

    def act_projection(act, ph):
        for j in ph.jobs:
            inputs_in(act, ph, j)
            if j["mm"]:
                act.wait_ge(ph.product, j["mm_count"])
            i = j["i"]
            if j["kind"] == "s":
                if i >= RING:
                    act.wait_ge(ph.stored[i % RING], 16 * (i // RING))
                nc.scalar.copy(split[0:j["m"], i % RING, 0, 0:j["n"]],
                               split_bank(ph, j) if j["mm"] else j["src"]).then_inc(ph.high, 1)
            else:
                r = i % ph.vring
                if i >= ph.vring:
                    act.wait_ge(ph.vstored[r], 16 * (i // ph.vring))
                s = value_bank(ph, j)
                if j["layer"] == 0:
                    v = s.rearrange("p (h d) -> p h d", d=D0)
                    nc.scalar.copy(vpad0[:, r, :, 0:31], v[:, :, 0:31])
                    nc.scalar.copy(vpad0[:, r, :, 32:41], v[:, :, 31:40]).then_inc(ph.padded, 1)
                else:
                    nc.scalar.copy(vpad1[:, r, :, 0:D1],
                                   s.rearrange("p (h d) -> p h d", d=D1)).then_inc(ph.padded, 1)

    def dve_projection(dve, ph, jobs=None):
        for j in ph.jobs if jobs is None else jobs:
            if j["kind"] == "s":
                i = j["i"]
                dve.wait_ge(ph.high, i + 1)
                nc.vector.tensor_tensor(split[0:j["m"], i % RING, 1, 0:j["n"]],
                                        split_bank(ph, j) if j["mm"] else j["src"],
                                        split[0:j["m"], i % RING, 0, 0:j["n"]].bitcast(F32),
                                        ALU.subtract).then_inc(ph.low, 1)

    def sp_projection(sp, ph, jobs=None):
        for j in ph.jobs if jobs is None else jobs:
            i = j["i"]
            if j["kind"] == "s":
                sp.wait_ge(ph.low, i + 1)
                sp.dma_start(j["dst"], split[0:j["m"], i % RING, :, 0:j["n"]].bitcast(F32)).then_inc(
                    ph.stored[i % RING], 16)
            else:
                sp.wait_ge(ph.padded, i + 1)
                pad = vpad0 if j["layer"] == 0 else vpad1
                sp.dma_start(j["dst"], pad[:, i % ph.vring, :, :].rearrange("p h w -> p (h w)").rearrange(
                    "p (g c) -> p g c", c=128)).then_inc(ph.vstored[i % ph.vring], 16)

    for a, (qd, kd, vd, dest) in ((A_MAIN, (q0_d, k0_d, v0_d, out_t)), (A_CA, (cq_d, x0_d, vx_d, ca_t)),
                                  (A_SELF, (q1_d, k1_d, v1_d, out_t)), (A_CROSS, (q2_d, k2_d, v2_d, out_t))):
        a.qd, a.kd, a.vd, a.dest = qd, kd, vd, dest
        n = a.name
        a.qk_loaded = [sem(f"{n}_qk_loaded{s}") for s in range(3)]
        a.v_loaded = [sem(f"{n}_v_loaded{s}") for s in range(3)]
        a.m_loaded = [sem(f"{n}_m_loaded{s}") for s in range(3)]
        a.score = sem(f"{n}_score")
        a.score_free = sem(f"{n}_score_free")
        a.neg_ready = sem(f"{n}_neg_ready")
        a.m_high = sem(f"{n}_m_high")
        a.pair = sem(f"{n}_pair")
        a.exp = sem(f"{n}_exp")
        a.used = sem(f"{n}_used")
        a.out_read = sem(f"{n}_out_read")
        a.norm = sem(f"{n}_norm")
        a.out_back = sem(f"{n}_out_back")
        a.out_done = sem(f"{n}_out_done")

    A_MAIN.ones, A_SELF.ones = sem("main_ones"), sem("self_ones")

    def q_view(a, s):
        return q_st[s][:, 0:a.g * a.nq].rearrange("p (j n) -> p j n", j=a.g)

    def k_view(a, s):
        kw = SK if a.keys > SQ else SQ
        return k_st[s][:, 0:a.g * kw].rearrange("p (j n) -> p j n", j=a.g)

    def item_index(a, g, i):
        if isinstance(g.loop, int) and g.loop * 3 + g.off == 0:
            return i, i % 3
        k = i - 1 + (1 if i >= a.per_step else 0)
        per = len(a.items) + 1
        return g.times(per, k), (g.off * per + k) % 3

    def flip_index(a, g):
        per = len(a.items) + 1
        last = isinstance(g.loop, int) and g.loop * 3 + g.off == a.groups - 1
        k = per - 1 + (0 if last else a.per_step)
        return g.times(per, k), (g.off * per + k) % 3

    def max_step(a, g, t):
        n = g.loop * 3 + g.off if isinstance(g.loop, int) else None
        ended = g.plus(-1) if t == 0 and n != 0 and (n is None or n <= a.groups) else None
        if n is not None and n >= a.groups:
            return (ended if n == a.groups else None), []
        return ended, [(i, a.items[i]) for i in range(t * a.per_step, (t + 1) * a.per_step)]

    def ahead(a, g, t):
        return g.plus((t + a.lead) // a.kt), (t + a.lead) % a.kt

    def run_groups(eng, a, body):
        with eng.Fori(0, a.loops) as r:
            for u in range(3):
                body(At(r, u))
        for n in range(3 * a.loops, a.groups):
            body(At(n // 3, n % 3))

    def sp_attention(sp, a, before, previous, side=None, kv_stored=None, values=None):
        if kv_stored is None:
            before.wait_stored(sp)
        else:
            kv_stored.wait_stored(sp)
        if a is A_MAIN:
            sp.wait_ge(a.ones, 1)
        if a is A_SELF:
            sp.wait_ge(a.ones, 2)
        kw = SK if a.keys > SQ else SQ
        rows = a.g * a.d

        def load_q(g):
            r0 = g.times(rows)
            s = g.slot
            for t, part in enumerate(a.terms_q):
                sp.dma_start(q_view(a, s)[t * a.d:(t + 1) * a.d, :, :].bitcast(F32),
                             a.qd[part, bass.ds(r0, rows), 0:a.nq].rearrange("(j d) n -> d j n", j=a.g)).then_inc(
                    a.qk_loaded[s], 16)

        def load_k(g):
            r0 = g.times(rows)
            s = g.slot
            for t, part in enumerate(a.terms_k):
                sp.dma_start(k_view(a, s)[t * a.d:(t + 1) * a.d, :, :].bitcast(F32),
                             a.kd[part, bass.ds(r0, rows), 0:kw].rearrange("(j d) n -> d j n", j=a.g)).then_inc(
                    a.qk_loaded[s], 16)

        def load_v(g):
            n = g.times(1)
            sp.dma_start(v_st[g.slot][:, 0:a.kt, :],
                         a.vd[bass.ds(n, 1), :, 0:a.kt, :].rearrange("o p t c -> (o p) t c")).then_inc(
                a.v_loaded[g.slot], 16)

        def load_m(g):
            sp.wait_ge(a.score_free, 3 + flip_index(a, g)[0] + 1)
            for part in range(2):
                sp.dma_start(q_st[g.slot][a.rows + part:a.rows + part + 1, 0:a.g * a.nq].bitcast(F32).rearrange(
                    "o (c n) -> o c n", n=a.qt), msplit[0:a.cols, g.slot, part, 0:a.qt].bitcast(F32)).then_inc(
                    a.m_loaded[g.slot], 16)

        for n in range(3):
            if previous is not None:
                last = max(x for x in range(previous.groups) if x % 3 == n) + 1
                steps = previous.kt * previous.pairs
                sp.wait_ge(previous.pair, last * steps)
            load_k(At(0, n))
            if kv_stored is None:
                load_q(At(0, n))
            if previous is not None:
                sp.wait_ge(previous.used, PRING + last * steps)
            if n == 0:
                (values or kv_stored or before).wait_vstored(sp)
            load_v(At(0, n))
        if kv_stored is not None:
            sp_projection(sp, before)
            before.wait_stored(sp)
            for n in range(3):
                load_q(At(0, n))
        if side is not None:
            for x in range(a.kt + 1):
                sp_projection(sp, side, share(side, x, a.lead))
        load_m(At(0, 0))
        if side is not None:
            for x in range(a.kt + 1, a.lead):
                sp_projection(sp, side, share(side, x, a.lead))

        def body(g):
            load_m(g.plus(1))
            sp.wait_ge(a.pair, g.times(a.kt * a.pairs, a.kt * a.pairs))
            load_k(g.plus(3))
            load_q(g.plus(3))
            sp.wait_ge(a.used, g.times(a.kt * a.pairs, PRING + a.kt * a.pairs))
            load_v(g.plus(3))

        loops = (a.groups - 3) // 3
        with sp.Fori(0, loops) as r:
            for u in range(3):
                body(At(r, u))
        for n in range(3 * loops, a.groups - 1):
            if n + 3 < a.groups:
                body(At(n // 3, n % 3))
            else:
                load_m(At((n + 1) // 3, (n + 1) % 3))

    def pe_attention(pe, a, side=None):
        steps = a.kt * a.pairs
        pe.sem_inc(a.used, PRING)

        def item(g, i, j, q, c):
            k, bank = item_index(a, g, i)
            if i == 0:
                pe.wait_ge(a.qk_loaded[g.slot], g.turn(16 * 2 * len(a.terms_q)))
            pe.wait_ge(a.score_free, k + 1)
            c0, cn = a.chunks[c]
            nc.tensor.matmul(PS[0:a.qt, SBANKS[bank], 0:cn],
                             q_view(a, g.slot)[0:a.rows, j, q * a.qt:(q + 1) * a.qt],
                             k_view(a, g.slot)[0:a.rows, j, c0:c0 + cn],
                             start=True, stop=True).then_inc(a.score, 1)

        def flip(ended):
            k, bank = flip_index(a, ended)
            pe.wait_ge(a.neg_ready, ended.times(1, 1))
            pe.wait_ge(a.score_free, k + 1)
            nc.tensor.transpose(PS[0:a.cols, SBANKS[bank], 0:a.qt],
                                negm[0:a.qt, ended.slot, 0:a.cols],
                                ident[0:a.qt, 0:a.qt]).then_inc(a.score, 1)

        def maxima(g, t, lo=0, hi=4):
            ended, items = max_step(a, g, t)
            start, stop = -(-lo * len(items) // 4), -(-hi * len(items) // 4)
            for i, jqc in items[start:stop]:
                item(g, i, *jqc)
            if ended is not None and (hi == 4 if items else lo == 0):
                flip(ended)

        def scores(g, t, p):
            sz = a.size[t]
            if t == 0 and p == 0:
                pe.wait_ge(a.m_loaded[g.slot], g.turn(32))
            q = g.times(steps, t * a.pairs + p)
            bank = 2 * ((g.off * steps + t * a.pairs + p) % 2)
            pe.wait_ge(a.exp, q + 1)
            for half in range(2):
                j = 2 * p + half
                mm = nc.tensor.matmul(PS[0:sz, bank + half, 0:a.nq],
                                      k_view(a, g.slot)[0:a.rows + 2, j, t * 128:t * 128 + sz],
                                      q_view(a, g.slot)[0:a.rows + 2, j, :], start=True, stop=True)
            mm.then_inc(a.pair, 1)

        def values(g, t, p):
            sz, w = a.size[t], a.width
            if t == 0 and p == 0:
                pe.wait_ge(a.v_loaded[g.slot], g.turn(16))
                pe.wait_ge(a.out_read, g.times(1, 1))
            q = g.times(steps, t * a.pairs + p)
            slot = (g.off * steps + t * a.pairs + p) % PRING
            pe.wait_ge(a.exp, q + 3)
            for half in range(2):
                j = 2 * p + half
                mm = nc.tensor.matmul(PS[w * j:w * j + w, OBANK, 0:a.nq],
                                      v_st[g.slot][0:sz, t, w * j:w * j + w],
                                      probs[0:sz, slot, half, 0:a.nq],
                                      start=(t == 0), stop=(t == a.kt - 1), tile_position=(0, w * j))
            mm.then_inc(a.used, 1)

        for x in range(a.lead):
            maxima(At(x // a.kt // 3, x // a.kt % 3), x % a.kt)
            if side is not None:
                pe_projection(pe, side, share(side, x, a.lead))
        if side is not None:
            pe.wait_ge(side.low, side.ns)
            pe.wait_ge(side.padded, side.nv)
        for p in range(a.pairs):
            scores(At(0, 0), 0, p)

        def body(g):
            last = isinstance(g.loop, int) and g.loop * 3 + g.off == a.groups - 1
            for t in range(a.kt):
                for p in range(a.pairs):
                    if t + 1 < a.kt:
                        scores(g, t + 1, p)
                    elif not last:
                        scores(g.plus(1), 0, p)
                    maxima(*ahead(a, g, t), *SPREAD[a.pairs][p])
                for p in range(a.pairs):
                    values(g, t, p)
                maxima(*ahead(a, g, t), *SPREAD[a.pairs][-1])

        run_groups(pe, a, body)

    def act_attention(act, a):
        act.sem_inc(a.exp, 2)

        def body(g):
            steps = a.kt * a.pairs
            for t in range(a.kt):
                for p in range(a.pairs):
                    x = g.off * steps + t * a.pairs + p
                    q = g.times(steps, t * a.pairs + p)
                    act.wait_ge(a.pair, q + 1)
                    act.wait_ge(a.used, q + 1)
                    nc.scalar.activation(probs[0:a.size[t], x % PRING, :, 0:a.nq],
                                         PS[0:a.size[t], 2 * (x % 2):2 * (x % 2) + 2, 0:a.nq],
                                         ACT.Exp, scale=a.scale).then_inc(a.exp, 1)

        run_groups(act, a, body)

    def dve_attention(dve, a, side=None):
        steps = a.kt * a.pairs
        nch = len(a.chunks)
        dve.sem_inc(a.score_free, 3)
        dve.sem_inc(a.out_read, 1)
        dve.sem_inc(a.out_back, 1)

        def maxima(g, t, normalising=None, done=0):
            ended, items = max_step(a, g, t)
            if ended is not None:
                k = item_index(a, ended, len(a.items) - 1)[0]
                dve.wait_ge(a.score_free, 3 + k + 1)
                nc.vector.tensor_reduce(negm[0:a.qt, ended.slot, 0:a.cols],
                                        maxp[0:a.qt, ended.slot, 0:a.cols * nch].rearrange("p (c k) -> p c k", k=nch),
                                        AX.X, ALU.max, negate=True).then_inc(a.neg_ready, 1)
            for n, (i, (j, q, c)) in enumerate(items):
                k, bank = item_index(a, g, i)
                dve.wait_ge(a.score, k + 1)
                nc.vector.tensor_reduce(maxp[0:a.qt, g.slot, i:i + 1], PS[0:a.qt, SBANKS[bank], 0:a.chunks[c][1]],
                                        AX.X, ALU.max).then_inc(a.score_free, 1)
                if normalising is not None:
                    normalise(normalising, done + n)
            if ended is not None:
                k, bank = flip_index(a, ended)
                dve.wait_ge(a.score, k + 1)
                src = PS[0:a.cols, SBANKS[bank], 0:a.qt]
                nc.vector.tensor_copy(msplit[0:a.cols, ended.slot, 0, 0:a.qt], src).then_inc(a.m_high, 1)
                dve.wait_ge(a.m_high, ended.times(1, 1))
                nc.vector.tensor_tensor(msplit[0:a.cols, ended.slot, 1, 0:a.qt], src,
                                        msplit[0:a.cols, ended.slot, 0, 0:a.qt].bitcast(F32),
                                        ALU.subtract).then_inc(a.score_free, 1)
            return done + len(items) if normalising is not None else 0

        def normalise(g, part):
            view = turned[:, 0:a.nq].rearrange("p (b r) -> p b r", r=32)
            if part == 0:
                dve.wait_ge(a.used, g.times(steps, PRING + steps))
                dve.wait_ge(a.out_back, g.times(1, 1))
                nc.vector.transpose(turned[:, 0:a.nq], PS[:, OBANK, 0:a.nq]).then_inc(a.out_read, 1)
            elif part == 1:
                dve.wait_ge(a.out_read, g.times(1, 2))
                nc.vector.reciprocal(recip[:, 0:a.nq // 32], view[:, :, 31]).then_inc(a.norm, 1)
            elif part == 2:
                dve.wait_ge(a.norm, g.times(2, 1))
                nc.vector.tensor_tensor(view, view, recip[:, 0:a.nq // 32].rearrange("p (b o) -> p b o", o=1)
                                        .to_broadcast([128, a.nq // 32, 32]), ALU.mult).then_inc(a.norm, 1)
            elif part == 3:
                dve.wait_ge(a.norm, g.times(2, 2))
                dve.wait_ge(a.out_done, g.times(1, 1))
                nc.vector.transpose(back[:, 0:a.nq], turned[:, 0:a.nq]).then_inc(a.out_back, 1)

        for x in range(a.lead + a.shift):
            maxima(At(x // a.kt // 3, x // a.kt % 3), x % a.kt)
            if side is not None and x < a.lead:
                dve_projection(dve, side, share(side, x, a.lead))

        def body(g):
            done = 0
            for t in range(a.kt):
                if t < a.kt - a.shift:
                    maxima(*ahead(a, g, t + a.shift))
                elif a.per_step > 1:
                    done = maxima(*ahead(a, g, t + a.shift), normalising=g, done=done)
                else:
                    normalise(g, done)
                    maxima(*ahead(a, g, t + a.shift))
                    normalise(g, done + 1)
                    done += 2
            for part in range(done, 4):
                normalise(g, part)

        run_groups(dve, a, body)

    class XValues:
        blank = sem("x_blank")
        padded = sem("x_padded")
        vstored = [sem(f"x_vstored{s}") for s in range(2)]

        def wait_vstored(self, eng):
            for s in range(2):
                eng.wait_ge(self.vstored[s], 16 * (TT // 2))

    x_values = XValues()

    def pool_x_values(pool):
        xv = x_values
        pool.wait_ge(first.low, first.ns)
        pool.wait_ge(first.padded, first.nv)
        nc.gpsimd.memset(xpad[:], 0.0).then_inc(xv.blank, 1)
        pool.wait_ge(xv.blank, 1)
        nc.gpsimd.memset(xpad[:, :, :, 31:32], 1.0)
        nc.gpsimd.memset(xpad[:, :, :, 63:64], 1.0).then_inc(xv.blank, 1)
        pool.wait_ge(loaded_x, 16)
        for t in range(TT):
            if t >= 2:
                pool.wait_ge(xv.vstored[t % 2], 16 * (t // 2))
            v = resid[:, t, :].rearrange("p (h d) -> p h d", d=D0)
            nc.gpsimd.tensor_copy(xpad[:, t % 2, :, 0:31], v[:, :, 0:31])
            nc.gpsimd.tensor_copy(xpad[:, t % 2, :, 32:41], v[:, :, 31:40]).then_inc(xv.padded, 1)
            pool.wait_ge(xv.blank, 2)
            pool.wait_ge(xv.padded, t + 1)
            b = t // 4
            nc.gpsimd.dma_start(vx_d[4 * b:4 * b + 4, :, t % 4, :].rearrange("g p c -> p g c"),
                                xpad[:, t % 2, :, :].rearrange("p h w -> p (h w)").rearrange(
                                    "p (g c) -> p g c", c=128)).then_inc(xv.vstored[t % 2], 16)

    def pool_outputs(pool, a):
        pool.sem_inc(a.out_done, 1)

        def body(g):
            pool.wait_ge(a.out_back, g.times(1, 2))
            nc.gpsimd.tensor_copy(a.dest[:, bass.ds(g.times(1), 1), 0:a.nq],
                                  back[:, 0:a.nq].rearrange("p (o n) -> p o n", o=1)).then_inc(a.out_done, 1)

        run_groups(pool, a, body)
        pool.wait_ge(a.out_done, 1 + a.groups)

    def pool_rows(pool, a):
        filled = a.d * len(a.terms_q)
        for s in range(3):
            m = nc.gpsimd.memset(k_st[s][96:128, :].bitcast(F32), 1.0)
        m.then_inc(a.ones, 1)
        pool.wait_ge(a.ones, 1)
        if filled < 96:
            for s in range(3):
                nc.gpsimd.memset(k_st[s][filled:96, :].bitcast(F32), 0.0)
                m = nc.gpsimd.memset(q_st[s][filled:96, :].bitcast(F32), 0.0)
            m.then_inc(a.ones, 1)
            pool.wait_ge(a.ones, 2)

    ca_prod, ca_evac = sem("ca_prod"), sem("ca_evac")
    ca_chain = sem("ca_chain")
    ca_ready = sem("ca_ready")

    def pe_ca_weights(pe):
        pe.wait_ge(first.low, first.ns)
        for b in range(B):
            for i, w in enumerate((w_kca, w_vca)):
                for m, (f0, fn) in enumerate(FTILES):
                    for k in range(CT):
                        c0 = b * SK + SK - NCA
                        mm = nc.tensor.matmul(PS[0:fn, 2 * b + i, 4 * m:4 * m + 4], w[0:CP, k, f0:f0 + fn],
                                              ctx_t[0:CP, k, c0:c0 + NCA], start=(k == 0), stop=(k == CT - 1))
                mm.then_inc(ca_prod, 1)
        pe.wait_ge(ca_evac, 4)
        for b in range(B):
            for m, (f0, fn) in enumerate(FTILES):
                mm = nc.tensor.matmul(PS[0:32, 2 * b, 0:D], vbd[0:fn, b, m, :, :].rearrange("p h t -> p (h t)"),
                                      w_s1[0:fn, m, :], start=(m == 0), stop=(m == KF - 1))
            mm.then_inc(ca_prod, 1)

    def dve_ca_weights(dve):
        for b in range(B):
            for i, dst in enumerate((kbd, vbd)):
                dve.wait_ge(ca_prod, 2 * b + i + 1)
                for m, (f0, fn) in enumerate(FTILES):
                    o = nc.vector.tensor_tensor(dst[0:fn, b, m, :, :],
                                                hmask[0:fn, m, :].rearrange("p (h t) -> p h t", t=NCA),
                                                PS[0:fn, 2 * b + i, 4 * m:4 * m + 4].rearrange(
                                                    "p (o t) -> p o t", o=1).to_broadcast([fn, H0, NCA]), ALU.mult)
                o.then_inc(ca_evac, 1)
        for b in range(B):
            dve.wait_ge(ca_prod, 4 + b + 1)
            nc.vector.tensor_copy(vw[:, b, :], PS[0:32, 2 * b, 0:D]).then_inc(ca_evac, 1)

    def pe_ca_tail(pe):
        for b in range(B):
            pe.wait_ge(A_CA.out_done, 1 + A_CA.groups)
            if b:
                pe.wait_ge(ca_ready, 5 * b)
            for m, (f0, fn) in enumerate(FTILES):
                for g in range(4):
                    mm = nc.tensor.matmul(PS[0:fn, m, 0:UQ], w_pad_b[:, g, f0:f0 + fn], ca_t[:, b * 4 + g, :],
                                          start=(g == 0), stop=(g == 3))
                mm.then_inc(ca_prod, 1)
            pe.wait_ge(ca_ready, 5 * b + 3)
            for h in range(2):
                for m, (f0, fn) in enumerate(FTILES):
                    mm = nc.tensor.matmul(PS[0:CP, 3, 32 * h:32 * h + 32], q2t[0:fn, m, 96 * h:96 * h + 96],
                                          kbd[0:fn, b, m, :, :].rearrange("p h t -> p (h t)"),
                                          start=(m == 0), stop=(m == KF - 1))
            mm.then_inc(ca_prod, 1)
            pe.wait_ge(ca_evac, 6 + 2 * b + 2)
            for h in range(2):
                mm = nc.tensor.matmul(PS[0:32, 4, 0:SQ], p3[:, b, h, :], onehot[:, h, :],
                                      start=(h == 0), stop=(h == 1))
            mm.then_inc(ca_prod, 1)

    def act_ca_tail(act):
        for b in range(B):
            for m, (f0, fn) in enumerate(FTILES):
                act.wait_ge(ca_prod, 6 + 5 * b + m + 1)
                nc.scalar.copy(q2t[0:fn, m, :], PS[0:fn, m, 0:UQ]).then_inc(ca_ready, 1)
            act.wait_ge(ca_evac, 6 + 2 * b + 1)
            nc.scalar.activation(p3[:, b, :, :], s3[:, :, :], ACT.Exp, scale=A_CA.scale).then_inc(ca_ready, 1)
            act.wait_ge(ca_prod, 6 + 5 * b + 5)
            nc.scalar.copy(ep3[:, b, :], PS[0:32, 4, 0:SQ]).then_inc(ca_ready, 1)

    def dve_ca_tail(dve):
        for b in range(B):
            dve.wait_ge(ca_prod, 6 + 5 * b + 4)
            view = "p h (g t) -> p (h g) t"
            s_in = PS[0:CP, 3, 0:64].rearrange("p (g t) -> p g t", t=NCA)
            m16 = recip[0:CP, 0:16]
            nc.vector.tensor_reduce(m16, s_in, AX.X, ALU.max).then_inc(ca_chain, 1)
            dve.wait_ge(ca_chain, 3 * b + 1)
            nc.vector.tensor_tensor(s3[:, :, :].rearrange(view, t=NCA), s_in,
                                    m16.rearrange("p (g o) -> p g o", o=1).to_broadcast([CP, 16, NCA]),
                                    ALU.subtract).then_inc(ca_evac, 1)
            dve.wait_ge(ca_ready, 5 * b + 4)
            e = p3[:, b, :, :].rearrange(view, t=NCA)
            nc.vector.tensor_reduce(recip[0:CP, 16:32], e, AX.X, ALU.add).then_inc(ca_chain, 1)
            dve.wait_ge(ca_chain, 3 * b + 2)
            nc.vector.reciprocal(recip[0:CP, 0:16], recip[0:CP, 16:32]).then_inc(ca_chain, 1)
            dve.wait_ge(ca_chain, 3 * b + 3)
            nc.vector.tensor_tensor(e, e, recip[0:CP, 0:16].rearrange("p (g o) -> p g o", o=1)
                                    .to_broadcast([CP, 16, NCA]), ALU.mult).then_inc(ca_evac, 1)

    class Join:

        def __init__(self, groups, w, bias, norm, ca):
            self.groups, self.w, self.bias, self.norm, self.ca = groups, w, bias, norm, ca
            self.base = norm * TT
            self.end = self.base + TT

        biased = sem("join_biased")
        product = sem("join_product")
        added = sem("join_added")
        chain = sem("join_chain")
        root = sem("join_root")
        normed = sem("join_normed")
        flipped = sem("join_flipped")
        ready = sem("join_ready")

    join0 = Join(4, w_pad_a, 0, 0, True)
    join1 = Join(5, w_pad_b, 1, 1, False)
    join2 = Join(5, w_pad_a, 2, 2, False)

    def pool_bias(pool, jn):
        for t in range(TT):
            o = nc.gpsimd.tensor_tensor(resid[:, t, :], resid[:, t, :], brows[:, jn.bias, :], ALU.add)
        o.then_inc(jn.biased, 1)

    def pe_join(pe, jn, a):
        pe.wait_ge(a.out_done, 1 + a.groups)
        if jn.ca:
            pe.wait_ge(ca_ready, 10)

        def product(t):
            b, c = t // 4, (t % 4) * 128
            if t >= 4:
                pe.wait_ge(jn.added, jn.base + t - 3)
            for g in range(jn.groups):
                mm = nc.tensor.matmul(PS[:, t % 4, 0:D], out_t[:, b * jn.groups + g, c:c + 128], jn.w[:, g, :],
                                      start=(g == 0), stop=(g == jn.groups - 1 and not jn.ca))
            if jn.ca:
                mm = nc.tensor.matmul(PS[:, t % 4, 0:D], ep3[:, b, c:c + 128], vw[:, b, :], start=False, stop=True)
            mm.then_inc(jn.product, 1)

        def flip(t):
            pe.wait_ge(jn.normed, jn.base + t + 1)
            if t >= 4:
                pe.wait_ge(jn.ready, jn.base + t - 3)
            for m, (f0, fn) in enumerate(FTILES):
                mm = nc.tensor.transpose(PS[0:fn, 4 + t % 4, 128 * m:128 * m + 128], xhat[:, t % 2, f0:f0 + fn],
                                         ident[:, :])
            mm.then_inc(jn.flipped, 1)

        for t in range(TT + 2):
            if t < TT:
                product(t)
            if t >= 2:
                flip(t - 2)

    def dve_join(dve, jn):
        dve.wait_ge(jn.biased, jn.norm + 1)
        for t in range(TT):
            dve.wait_ge(jn.product, jn.base + t + 1)
            nc.vector.tensor_tensor(resid[:, t, :], PS[:, t % 4, 0:D], resid[:, t, :], ALU.add).then_inc(jn.added, 1)
            dve.wait_ge(jn.added, jn.base + t + 1)
            nc.vector.bn_stats(stats[:, :], resid[:, t, :]).then_inc(jn.chain, 1)
            dve.wait_ge(jn.chain, 3 * (jn.base + t) + 1)
            nc.vector.bn_aggr(mv[:, t, :], stats[:, :]).then_inc(jn.chain, 1)
            dve.wait_ge(jn.chain, 3 * (jn.base + t) + 2)
            dve.wait_ge(jn.root, jn.base + t + 1)
            nc.vector.reciprocal(rstd[:, t:t + 1], std[:, t:t + 1]).then_inc(jn.chain, 1)
            dve.wait_ge(jn.chain, 3 * (jn.base + t) + 3)
            if t >= 2:
                dve.wait_ge(jn.flipped, jn.base + t - 1)
            nc.vector.tensor_scalar(xhat[:, t % 2, :], resid[:, t, :], mv[:, t, 0:1], rstd[:, t:t + 1],
                                    ALU.subtract, ALU.mult).then_inc(jn.normed, 1)

    def act_join(act, jn):
        def flipped(t):
            act.wait_ge(jn.flipped, jn.base + t + 1)
            for m, (f0, fn) in enumerate(FTILES):
                c = 6 * jn.norm + m
                o = nc.scalar.activation(act_t[0:fn, m, t * 128:(t + 1) * 128],
                                         PS[0:fn, 4 + t % 4, 128 * m:128 * m + 128], ACT.Identity,
                                         bias=params[0:fn, c + 3:c + 4], scale=params[0:fn, c:c + 1])
            o.then_inc(jn.ready, 1)

        for t in range(TT + 1):
            if t < TT:
                act.wait_ge(jn.chain, 3 * (jn.base + t) + 2)
                nc.scalar.activation(std[:, t:t + 1], mv[:, t, 1:2], ACT.Sqrt, bias=eps[:, :]).then_inc(jn.root, 1)
            if t:
                flipped(t - 1)

    w1_loaded, w2_loaded = sem("w1_loaded"), sem("w2_loaded")
    ff_product, ff_gelu, ff_inner = sem("ff_product"), sem("ff_gelu"), sem("ff_inner")
    split_high, split_low = sem("split_high"), sem("split_low")
    ff_biased, ff_down, ff_out, out_stored = sem("ff_biased"), sem("ff_down"), sem("ff_out"), sem("out_stored")

    def w1_part(w, m):
        return w[:, :, :].rearrange("p k (v f) -> p k v f", v=2)[:, :, :, m * 128:(m + 1) * 128]

    def ff_parts(kind, x):
        if kind == "act":
            return [w[:, 0:2, x * SQ:(x + 1) * SQ] for w in (act_t, act_high, act_low)]
        if kind == "rest":
            return [w[0:64, 2, x * SQ:(x + 1) * SQ] for w in (act_t, act_high, act_low)]
        if kind == "w1":
            return [w1_part(w, x) for w in (w1_raw, w1_high, w1_low)]
        if kind == "w2":
            return [w[:, x, :] for w in (w2_raw, w2_high, w2_low)]
        return [w[:, x % FT, :] for w in (ff_raw, ff_high, ff_low)]

    def after_inner(i):
        parts = []
        if i < FT:
            parts += [("w1", i + 2)] if i + 2 < FT else []
            parts += [("w2", i)]
        if i == 4:
            parts += [("act", 1), ("rest", 1)]
        return parts

    BEFORE = [("act", 0), ("rest", 0), ("w1", 0), ("w1", 1)]
    FF_SPLITS = BEFORE + [p for i in range(B * FT) for p in after_inner(i) + [("inner", i)]]

    def is_split(kind, x):
        return FF_SPLITS.index((kind, x)) + 1

    def act_split(act, kind, x):
        raw, high, low = ff_parts(kind, x)
        if kind == "w1":
            act.wait_ge(w1_loaded, 16)
        if kind == "w2":
            act.wait_ge(w2_loaded, 16)
        if kind == "inner":
            act.wait_ge(ff_inner, x + 1)
        if kind == "act":
            act.wait_ge(join2.ready, join2.end)
        nc.scalar.copy(high, raw).then_inc(split_high, 1)

    def dve_split(dve, kind, x):
        raw, high, low = ff_parts(kind, x)
        dve.wait_ge(split_high, is_split(kind, x))
        nc.vector.tensor_tensor(low, raw, high.bitcast(F32), ALU.subtract).then_inc(split_low, 1)

    def pe_ff(pe):
        def up(i):
            half, m = i // FT, i % FT
            if m == 0:
                pe.wait_ge(split_low, is_split("rest", half))
            if half == 0:
                pe.wait_ge(split_low, is_split("w1", m))
            if i >= 2:
                pe.wait_ge(ff_inner, i - 1)
            cols = slice(half * SQ, (half + 1) * SQ)
            for part in range(2):
                f0 = part * FF + m * 128
                for k, p in enumerate(XP):
                    for n, (w, a) in enumerate(((w1_high, act_high), (w1_high, act_low), (w1_low, act_high))):
                        mm = nc.tensor.matmul(PS[:, 2 * (i % 2) + part, :], w[0:p, k, f0:f0 + 128], a[0:p, k, cols],
                                              start=(k == 0 and n == 0), stop=(k == KF - 1 and n == 2))
            mm.then_inc(ff_product, 1)

        def down(t):
            if t % 4 == 0:
                pe.wait_ge(split_low, is_split("inner", FT * (t // 4 + 1) - 1))
            if t >= 4:
                pe.wait_ge(ff_out, t - 3)
            rows = slice((t % 4) * 128, (t % 4 + 1) * 128)
            for m in range(FT):
                for n, (a, w) in enumerate(((ff_high, w2_high), (ff_high, w2_low), (ff_low, w2_high))):
                    mm = nc.tensor.matmul(PS[:, 4 + t % 4, 0:D], a[:, m, rows], w[:, m, :],
                                          start=(m == 0 and n == 0), stop=(m == FT - 1 and n == 2))
            mm.then_inc(ff_down, 1)

        for i in range(FT + 2):
            up(i)
        for t in range(4):
            down(t)
        for i in range(FT + 2, 2 * FT):
            up(i)
        for t in range(4, TT):
            down(t)

    def act_ff(act):
        for part in BEFORE:
            act_split(act, *part)
        for i in range(B * FT):
            act.wait_ge(ff_product, i + 1)
            if i >= 2:
                act.wait_ge(ff_inner, i - 1)
            c = 18 + FT + i % FT
            nc.scalar.activation(gelu[:, i % 2, :], PS[:, 2 * (i % 2) + 1, :], ACT.Gelu,
                                 bias=params[:, c:c + 1]).then_inc(ff_gelu, 1)
            for part in after_inner(i):
                act_split(act, *part)
            act_split(act, "inner", i)

    def dve_ff(dve):
        def result(t):
            dve.wait_ge(ff_down, t + 1)
            nc.vector.tensor_tensor(resid[:, t, :], PS[:, 4 + t % 4, 0:D], resid[:, t, :], ALU.add).then_inc(ff_out, 1)

        for part in BEFORE:
            dve_split(dve, *part)
        for i in range(B * FT):
            m = i % FT
            if i == FT:
                dve.wait_ge(ff_biased, 1)
                for t in range(4):
                    result(t)
            dve.wait_ge(ff_gelu, i + 1)
            nc.vector.scalar_tensor_tensor(out=ff_raw[:, m, :], in0=PS[:, 2 * (i % 2), :],
                                           scalar=params[:, 18 + m:19 + m], in1=gelu[:, i % 2, :],
                                           op0=ALU.add, op1=ALU.mult).then_inc(ff_inner, 1)
            for part in after_inner(i):
                dve_split(dve, *part)
            dve_split(dve, "inner", i)
        for t in range(4, TT):
            result(t)

    pads_zero, pads_set = sem("pads_zero"), sem("pads_set")
    block = nc.Block()
    with block:

        @block.sync
        def _(sp):
            for dst, name in loads["a"]:
                sp.dma_start(dst[:], ins[name]).then_inc(loaded_a, 16)
            for dst, name in loads["c"]:
                sp.dma_start(dst[:], ins[name]).then_inc(loaded_c, 16)
            for dst, name in loads["x"]:
                sp.dma_start(dst[:], ins[name]).then_inc(loaded_x, 16)
            sp_projection(sp, first, first.jobs[:C_FROM])
            later = first.jobs[C_FROM:]
            for n, (dst, name) in enumerate(loads["b"]):
                sp_projection(sp, first, later[2 * n:2 * n + 2])
                sp.dma_start(dst[:], ins[name]).then_inc(loaded_b, 16)
            sp.dma_start(brows[:].rearrange("p a d -> p (a d)"), ins["brows"].partition_broadcast(128)).then_inc(loaded_b, 16)
            sp_projection(sp, first, later[2 * len(loads["b"]):])
            sp_attention(sp, A_MAIN, first, None, side=second)
            sp.wait_ge(ca_evac, 6)
            for dst, name in ((w_s0, "q1"), (w_s1, "k1")):
                sp.dma_start(dst[:], ins[name]).then_inc(loaded_b, 16)
            sp_attention(sp, A_CA, first, A_MAIN, values=x_values)
            sp.wait_ge(ca_prod, 6 + 10)
            sp.dma_start(w_pad_b[:], ins["o1_g"]).then_inc(loaded_b, 16)
            sp.wait_ge(join0.product, join0.end)
            sp.dma_start(w_pad_a[:], ins["o2_g"]).then_inc(loaded_b, 16)
            sp_projection(sp, selfp)
            sp.wait_ge(selfp.padded, selfp.nv)
            sp.dma_start(w_s0[:], ins["q2"]).then_inc(loaded_b, 16)
            sp_attention(sp, A_SELF, selfp, A_CA)
            sp_attention(sp, A_CROSS, crossp, A_SELF, kv_stored=second)
            sp.wait_ge(A_CROSS.out_done, 1 + A_CROSS.groups)
            sp.dma_start(w1_raw[:], ins["ff_w1"]).then_inc(w1_loaded, 16)
            sp.wait_ge(join2.product, join2.end)
            sp.dma_start(w2_raw[:], ins["ff_w2"]).then_inc(w2_loaded, 16)
            for t in range(TT):
                sp.wait_ge(ff_out, t + 1)
                sp.dma_start(out_dram[t * 128:(t + 1) * 128, :], resid[:, t, :]).then_inc(out_stored, 16)
            sp.wait_ge(out_stored, 16 * TT)

        @block.tensor
        def _(pe):
            pe.wait_ge(loaded_a, ALL_A)
            pe_projection(pe, first)
            pe.wait_ge(loaded_b, ALL_B)
            pe_ca_weights(pe)
            pe.wait_ge(ca_evac, 6)
            pe.wait_ge(first.padded, first.nv)
            pe_attention(pe, A_MAIN, side=second)
            pe.wait_ge(A_MAIN.out_read, 1 + A_MAIN.groups)
            pe_attention(pe, A_CA)
            pe_ca_tail(pe)
            pe_join(pe, join0, A_MAIN)
            pe.wait_ge(loaded_b, ALL_B + 16 * 4)
            pe.wait_ge(join0.ready, join0.end)
            pe_projection(pe, selfp)
            pe.wait_ge(selfp.low, selfp.ns)
            pe.wait_ge(selfp.padded, selfp.nv)
            pe_attention(pe, A_SELF)
            pe_join(pe, join1, A_SELF)
            pe.wait_ge(loaded_b, ALL_B + 16 * 5)
            pe.wait_ge(join1.ready, join1.end)
            pe_projection(pe, crossp)
            pe.wait_ge(crossp.low, crossp.ns)
            pe_attention(pe, A_CROSS)
            pe_join(pe, join2, A_CROSS)
            pe_ff(pe)

        @block.scalar
        def _(act):
            act.wait_ge(loaded_a, ALL_A)
            act.wait_ge(pads_set, 1)
            act_projection(act, first)
            act.wait_ge(loaded_b, ALL_B)
            first.wait_stored(act)
            act_projection(act, second)
            second.wait_stored(act)
            act_attention(act, A_MAIN)
            act_attention(act, A_CA)
            act_ca_tail(act)
            act_join(act, join0)
            act_projection(act, selfp)
            act_attention(act, A_SELF)
            act_join(act, join1)
            act_projection(act, crossp)
            act_attention(act, A_CROSS)
            act_join(act, join2)
            act_ff(act)

        @block.vector
        def _(dve):
            dve.wait_ge(loaded_a, ALL_A)
            dve_projection(dve, first)
            dve.wait_ge(loaded_b, ALL_B)
            dve_ca_weights(dve)
            dve_attention(dve, A_MAIN, side=second)
            dve_attention(dve, A_CA)
            dve_ca_tail(dve)
            dve_join(dve, join0)
            dve_projection(dve, selfp)
            dve_attention(dve, A_SELF)
            dve_join(dve, join1)
            dve_projection(dve, crossp)
            dve_attention(dve, A_CROSS)
            dve_join(dve, join2)
            dve_ff(dve)

        @block.gpsimd
        def _(pool):
            nc.gpsimd.memset(eps[:], EPS)
            nc.gpsimd.memset(vpad0[:], 0.0)
            nc.gpsimd.memset(vpad1[:], 0.0).then_inc(pads_zero, 1)
            pool.wait_ge(pads_zero, 1)
            nc.gpsimd.memset(vpad0[:, :, :, 31:32], 1.0)
            nc.gpsimd.memset(vpad0[:, :, :, 63:64], 1.0)
            nc.gpsimd.memset(vpad1[:, :, :, 31:32], 1.0).then_inc(pads_set, 1)
            pool.wait_ge(pads_set, 1)
            pool_rows(pool, A_MAIN)
            pool_x_values(pool)
            pool.wait_ge(loaded_b, ALL_B)
            pool_bias(pool, join0)
            pool_outputs(pool, A_MAIN)
            pool_outputs(pool, A_CA)
            pool.wait_ge(A_CA.pair, A_CA.groups * A_CA.kt * A_CA.pairs)
            pool_rows(pool, A_SELF)
            pool.wait_ge(join0.normed, join0.end)
            pool_bias(pool, join1)
            pool_outputs(pool, A_SELF)
            pool.wait_ge(join1.normed, join1.end)
            pool_bias(pool, join2)
            pool_outputs(pool, A_CROSS)
            pool.wait_ge(join2.normed, join2.end)
            for t in range(TT):
                o = nc.gpsimd.tensor_tensor(resid[:, t, :], resid[:, t, :], brows[:, 3, :], ALU.add)
            o.then_inc(ff_biased, 1)


def kernel(**inputs):
    import numpy as _np
    import concourse.bacc as _bacc
    from concourse import mybir as _mybir
    from concourse.bass_utils import run_bass_kernel_spmd as _run

    i = {k: _np.asarray(v) for k, v in inputs.items()}

    def tiles(a, p=128):
        n = -(-a.shape[0] // p)
        full = _np.zeros((n * p, a.shape[1]), a.dtype)
        full[:a.shape[0]] = a
        return full.reshape(n, p, a.shape[1]).transpose(1, 0, 2)

    def by_group(w, heads, d, width):
        g = 128 // width
        full = _np.zeros((heads // g, 128, w.shape[1]), w.dtype)
        for h in range(heads):
            r = width * (h % g)
            full[h // g, r:r + min(d, 31)] = w[h * d:h * d + min(d, 31)]
            if d > 31:
                full[h // g, r + 32:r + 32 + d - 31] = w[h * d + 31:(h + 1) * d]
        if heads // g < 5:
            full = _np.concatenate([full, _np.zeros((5 - heads // g, 128, w.shape[1]), w.dtype)])
        return full.transpose(1, 0, 2)

    x = i["x"].reshape(TOK, D)
    ctx = i["ctx_768"].reshape(B * SK, DC)
    L0, L1 = "L0_xattn_", "L1_xattn_"
    f32 = x.dtype
    one = _np.zeros((UQ, SQ), f32)
    one[_np.linspace(0, DC - 1, SQ).astype(_np.int64), _np.arange(SQ)] = 1.0
    mask = _np.zeros((D, H0, NCA), f32)
    for h in range(H0):
        mask[h * D0:(h + 1) * D0, h] = 1.0
    cols = [tiles(i[L1 + n][:, None])[:, :, 0] for n in ("n1_g", "n1_b", "n2_g", "n2_b", "n3_g", "n3_b", "ff_b1")]
    feed = {
        "x_t": tiles(x.T), "x": tiles(x), "ctx_t": tiles(ctx.T, CP),
        "ca": i["ctx_768"][:, SK - NCA:].transpose(1, 0, 2),
        "Wq": tiles(i[L0 + "Wq"]), "Wout": tiles(i[L0 + "Wout"]),
        "Wk": tiles(i[L0 + "Wk"], CP), "Wv": tiles(i[L0 + "Wv"], CP),
        "Wk_ca": tiles(i[L0 + "Wk_ca"], CP), "Wv_ca": tiles(i[L0 + "Wv_ca"], CP), "Wq_ca": i[L0 + "Wq_ca"],
        "Wq_g": by_group(i[L0 + "Wq"], H0, D0, 64), "Wout_g": by_group(i[L0 + "Wout"], H0, D0, 64),
        "q1": tiles(i[L1 + "q1"]), "k1": tiles(i[L1 + "k1"]), "v1": tiles(i[L1 + "v1"]), "q2": tiles(i[L1 + "q2"]),
        "k2": tiles(i[L1 + "k2"], CP), "v2": tiles(i[L1 + "v2"], CP),
        "o1_g": by_group(i[L1 + "o1_w"], H1, D1, 32), "o2_g": by_group(i[L1 + "o2_w"], H1, D1, 32),
        "ff_w1": tiles(i[L1 + "ff_w1"]), "ff_w2": tiles(i[L1 + "ff_w2"]),
        "params": _np.concatenate(cols, axis=1),
        "brows": _np.concatenate([i[L0 + "b_out"], i[L1 + "o1_b"], i[L1 + "o2_b"], i[L1 + "ff_b2"]]),
        "onehot": tiles(one, CP), "hmask": tiles(mask.reshape(D, H0 * NCA)), "ident": _np.eye(128, dtype=f32),
    }
    nc = _bacc.Bacc("TRN2", target_bir_lowering=False, num_devices=1)
    arrays, args = {}, {}
    for name, a in feed.items():
        a = _np.ascontiguousarray(a)
        arrays[f"in_{name}"] = a
        args[name] = nc.dram_tensor(f"in_{name}", a.shape, _mybir.dt.from_np(a.dtype), kind="ExternalInput").ap()
    out = nc.dram_tensor("out_0", (TOK, D), _mybir.dt.float32, kind="ExternalOutput").ap()
    build(nc, args, out)
    r = _run(nc, [arrays], core_ids=[0])
    return r.results[0]["out_0"].reshape(B, SQ, D)
```
